# Optimizing a Trainium2 kernel written in Bass

```python
import numpy as np
import jax
import jax.numpy as jnp

def _softmax(x, axis=-1):
    return jax.nn.softmax(x, axis=axis)

def _gelu(x):
    return jax.nn.gelu(x, approximate=True)

def _silu(x):
    return jax.nn.silu(x)

def _sigmoid(x):
    return jax.nn.sigmoid(x)

def _layernorm(x, axis=-1, eps=1e-05):
    m = jnp.mean(x, axis=axis, keepdims=True)
    v = jnp.var(x, axis=axis, keepdims=True)
    return (x - m) / jnp.sqrt(v + eps)

def _scatter_add(tgt, idx, src, axis=0):
    return tgt.at[idx].add(src)

def _segment_sum(src, seg, n):
    return jax.ops.segment_sum(src, seg, n)
kernel_name = 'mk_gnn_resnorm_d1_gnn_r8_930787'

def setup_inputs(seed: int=0):
    np.random.seed(seed)
    _w = jnp.asarray

    def _rec_inputs():
        import jax
        import jax.numpy as jnp
        _gk = jax.random.key(seed)
        x = -0.0003713 + 1 * jax.random.normal(jax.random.fold_in(_gk, 1), (6250, 128), jnp.float32)
        _s = jax.random.randint(jax.random.fold_in(_gk, 2), (100000,), 0, 6250, jnp.int32)
        _d = jax.random.randint(jax.random.fold_in(_gk, 3), (100000,), 0, 6250, jnp.int32)
        _loop = jnp.arange(6250, dtype=jnp.int32)
        src = jnp.concatenate([_s, _d, _loop])
        dst = jnp.concatenate([_d, _s, _loop])
        _o = jnp.argsort(dst, stable=True)
        src = src[_o]
        dst = dst[_o]
        edge_attr_128 = 0.000189758 + 1.00013 * jax.random.normal(jax.random.fold_in(_gk, 11), (206250, 128), jnp.float32)
        return (x, src, dst, edge_attr_128)
    x, src, dst, edge_attr_128 = _rec_inputs()

    def _L0_gnn_setup():
        import jax, jax.numpy as jnp
        import numpy as np
        EPS = 1e-05
        key = jax.random.key(seed)
        ks = jax.random.split(key, 10)
        N, E, D = (12500, 50000, 128)
        H = 2 * D
        x = jax.random.normal(ks[0], (N, D), dtype=jnp.float32)
        edge_index = jax.random.randint(ks[1], (2, E), 0, N, dtype=jnp.int64)
        edge_attr = jax.random.normal(ks[2], (E, D), dtype=jnp.float32)
        s = 1.0 / np.sqrt(D)
        W1 = jax.random.uniform(ks[3], (D, H), jnp.float32, -s, s)
        b1 = jnp.zeros((H,), jnp.float32)
        W2 = jax.random.uniform(ks[4], (H, D), jnp.float32, -1.0 / np.sqrt(H), 1.0 / np.sqrt(H))
        b2 = jnp.zeros((D,), jnp.float32)
        ln_w = jnp.ones((D,), jnp.float32)
        ln_b = jnp.zeros((D,), jnp.float32)
        gn_w = jnp.ones((D,), jnp.float32)
        gn_b = jnp.zeros((D,), jnp.float32)
        gn_ms = jnp.ones((D,), jnp.float32)
        return {'x': x, 'edge_index': edge_index, 'edge_attr': edge_attr, 'W1': W1, 'b1': b1, 'W2': W2, 'b2': b2, 'ln_w': ln_w, 'ln_b': ln_b, 'gn_w': gn_w, 'gn_b': gn_b, 'gn_ms': gn_ms}
    _L0_gnn_all = _L0_gnn_setup()
    _L0_gnn_in = {k: v for k, v in _L0_gnn_all.items() if k in ('W1', 'b1', 'W2', 'b2', 'ln_w', 'ln_b', 'gn_w', 'gn_b', 'gn_ms')}
    del _L0_gnn_all
    return {'x': x, 'src': src, 'dst': dst, 'edge_attr_128': edge_attr_128, 'L0_gnn_W1': _L0_gnn_in['W1'], 'L0_gnn_b1': _L0_gnn_in['b1'], 'L0_gnn_W2': _L0_gnn_in['W2'], 'L0_gnn_b2': _L0_gnn_in['b2'], 'L0_gnn_ln_w': _L0_gnn_in['ln_w'], 'L0_gnn_ln_b': _L0_gnn_in['ln_b'], 'L0_gnn_gn_w': _L0_gnn_in['gn_w'], 'L0_gnn_gn_b': _L0_gnn_in['gn_b'], 'L0_gnn_gn_ms': _L0_gnn_in['gn_ms']}

def reference(x, src, dst, edge_attr_128, L0_gnn_W1, L0_gnn_b1, L0_gnn_W2, L0_gnn_b2, L0_gnn_ln_w, L0_gnn_ln_b, L0_gnn_gn_w, L0_gnn_gn_b, L0_gnn_gn_ms):
    import jax
    import jax.numpy as jnp

    def _L0_gnn_ref(x, edge_index, edge_attr, W1, b1, W2, b2, ln_w, ln_b, gn_w, gn_b, gn_ms):
        import jax, jax.numpy as jnp
        import numpy as np
        EPS = 1e-05
        N = x.shape[0]
        src, dst = (edge_index[0], edge_index[1])
        msg = x[src] + edge_attr
        agg = jax.ops.segment_sum(msg, dst, num_segments=N)
        h = jax.nn.relu(agg @ W1 + b1) @ W2 + b2
        mu = jnp.mean(h)
        var = jnp.mean((h - mu) ** 2)
        h = (h - mu) * jax.lax.rsqrt(var + EPS) * ln_w + ln_b
        mean = jnp.mean(h, axis=0)
        sub = h - gn_ms * mean
        gvar = jnp.mean(sub ** 2, axis=0)
        h = sub * jax.lax.rsqrt(gvar + EPS) * gn_w + gn_b
        h = jax.nn.gelu(h)
        return h + x
    edge_index = jnp.stack([src, dst])
    x = _layernorm(x + _L0_gnn_ref(x, edge_index, edge_attr_128, L0_gnn_W1, L0_gnn_b1, L0_gnn_W2, L0_gnn_b2, L0_gnn_ln_w, L0_gnn_ln_b, L0_gnn_gn_w, L0_gnn_gn_b, L0_gnn_gn_ms), axis=-1)
    return x

_drawn_inputs = setup_inputs


def setup_inputs(seed=0):
    import zlib

    import numpy as np

    out = dict(_drawn_inputs(seed))
    spreads = {'L0_gnn_b1': (0.0, 0.8),
     'L0_gnn_b2': (0.0, 0.8),
     'L0_gnn_ln_w': (1.0, 0.6),
     'L0_gnn_ln_b': (0.0, 0.8),
     'L0_gnn_gn_w': (1.0, 0.2),
     'L0_gnn_gn_b': (0.0, 0.1),
     'L0_gnn_gn_ms': (1.0, 0.2)}
    factors = {}
    for name, (base, spread) in spreads.items():
        noise = np.random.default_rng([zlib.crc32(name.encode()), seed]).standard_normal(out[name].shape)
        drawn = base * np.exp(spread * noise) if base else spread * noise
        out[name] = jnp.asarray(drawn.astype(out[name].dtype))
    for name, factor in factors.items():
        out[name] = (out[name] * factor).astype(out[name].dtype)
    return out
```

```python
from contextlib import ExitStack

import concourse.bass as bass
from concourse import mybir

ALU = mybir.AluOpType
ACT = mybir.ActivationFunctionType
F32 = mybir.dt.float32
I32 = mybir.dt.int32
AX_X = mybir.AxisListType.X

P = 128
EPS = 1e-5
TILES = 16
GROUP = P * TILES
WINDOW = 80
SLOTS = 4
CHUNK = 250
BLOCK = 4
PAD = 1.0e6


def gnn_kernel(nc, x, src, dst, edge_attr, W1, b1, W2, b2, ln_w, ln_b, gn_w, gn_b, gn_ms, out):
    N, D = x.shape
    E = src.shape[0]
    H = W1.shape[1]
    HC = H // P
    FULL = E // GROUP
    REST = E - FULL * GROUP
    REST_P, REST_E = REST // TILES, REST % TILES
    GROUPS = FULL + 1
    assert D == P and REST and REST_E and FULL % SLOTS == 0 and GROUPS <= P
    PASSES = -(-N // WINDOW)
    CHUNKS = N // CHUNK
    assert CHUNKS * CHUNK == N and CHUNKS % 2 == 1
    NT = -(-N // P)
    LAST = N - (NT - 1) * P
    BLOCKS = (NT - 1) // BLOCK
    assert BLOCKS * BLOCK == NT - 1 and BLOCKS % 2 == 0

    with ExitStack() as ctx:
        def sb(name, shape, dt=F32):
            return ctx.enter_context(nc.sbuf_tensor(name, shape, dt))

        def psum(name, shape, dt=F32):
            return ctx.enter_context(nc.psum_tensor(name, shape, dt))

        def sem(name):
            return ctx.enter_context(nc.semaphore(name))

        edges = sb("edges", [P, SLOTS, TILES * D])
        gathered = sb("gathered", [P, SLOTS, TILES * D])
        src_slot = sb("src_slot", [P, SLOTS, TILES], I32)
        onehot = sb("onehot", [P, 2, TILES * WINDOW])
        dst_rows = sb("dst_rows", [P, GROUP], I32)
        src_rows = sb("src_rows", [P, GROUP], I32)
        rows_f = gathered[:, SLOTS - 2:SLOTS, :]
        pad_f = sb("pad_f", [P, GROUP - REST])
        src_cols = sb("src_cols", [P, TILES, P], I32)
        dst_cols = sb("dst_cols", [P, TILES, P])
        agg = sb("agg", [P, N + WINDOW])
        h = sb("h", [P, N])
        hidden = sb("hidden", [P, 2, HC, CHUNK])
        gelu = sb("gelu", [P, 2, BLOCK * P])
        xs = sb("xs", [P, NT, D])
        w1 = sb("w1", [P, H])
        w2 = sb("w2", [P, HC, D])
        b1c = sb("b1c", [P, HC])
        par = sb("par", [P, 6])
        B2, LNW, LNB, GNW, GNB, GNM = range(6)
        iota_i = sb("iota_i", [P, P], I32)
        iota_f = sb("iota_f", [P, P])
        prow_i = sb("prow_i", [P, 1], I32)
        prow_f = sb("prow_f", [P, 1])
        ident = sb("ident", [P, P])
        ones = sb("ones", [P, P])
        lo = sb("lo", [P, 1])
        hi = sb("hi", [P, 1])
        diag = sb("diag", [P, 2, P])
        base_f = sb("base_f", [P, P])
        base_i = sb("base_i", [1, P], I32)
        wide = sb("wide", [P, 1])
        narrow = sb("narrow", [P, 1])
        wide_i = sb("wide_i", [1, 1], I32)
        stats = sb("stats", [P, CHUNKS, 6])
        mv = sb("mv", [P, 2])
        st = sb("st", [P, 24])
        lnstats = sb("lnstats", [P, NT, 6])
        lnmean = sb("lnmean", [P, NT])
        lngap = sb("lngap", [P, NT])
        rstd = sb("rstd", [P, NT])

        sums = [psum(f"sums{i}", [P, 512]) for i in range(2)]
        zps = [psum(f"zps{i}", [P, HC, 256]) for i in range(2)]
        hps = [psum(f"hps{i}", [P, 512]) for i in range(2)]
        tps = [psum(f"tps{i}", [P, 512]) for i in range(2)]

        rows_padded = sem("rows_padded")
        dst_loaded = sem("dst_loaded")
        src_loaded = sem("src_loaded")
        consts_ready = sem("consts_ready")
        setup = sem("setup")
        diag_ready = sem("diag_ready")
        base_summed = sem("base_summed")
        rows_ready = sem("rows_ready")
        turned = sem("turned")
        turned_free = sem("turned_free")
        cols_ready = sem("cols_ready")
        mode_ready = sem("mode_ready")
        edge_loaded = [sem(f"edge_loaded{i}") for i in range(SLOTS)]
        tail_loaded = sem("tail_loaded")
        gather_done = [sem(f"gather_done{i}") for i in range(SLOTS)]
        indices_ready = sem("indices_ready")
        gather_begun = sem("gather_begun")
        pass_begun = sem("pass_begun")
        onehot_ready = sem("onehot_ready")
        slots_free = sem("slots_free")
        sums_free = sem("sums_free")
        shifted = sem("shifted")
        agg_ready = sem("agg_ready")
        weights_loaded = sem("weights_loaded")
        params_loaded = sem("params_loaded")
        x_loaded = sem("x_loaded")
        z_ready = sem("z_ready")
        hidden_ready = sem("hidden_ready")
        h_summed = sem("h_summed")
        h_ready = sem("h_ready")
        h_stats = sem("h_stats")
        norm = sem("norm")
        mean_in = sem("mean_in")
        mean_summed = sem("mean_summed")
        affine_ready = sem("affine_ready")
        act_ready = sem("act_ready")
        out_turned = sem("out_turned")
        y_ready = sem("y_ready")
        ln_stats = sem("ln_stats")
        ln = sem("ln")
        root_in = sem("root_in")
        root_out = sem("root_out")
        out_ready = sem("out_ready")
        out_stored = sem("out_stored")

        edge_full = edge_attr[0:FULL * GROUP, :].rearrange("(g p j) d -> g p (j d)", p=P, j=TILES)
        rest0 = FULL * GROUP
        edge_rest = edge_attr[rest0:rest0 + REST_P * TILES, :].rearrange("(p j) d -> p (j d)", j=TILES)
        edge_last = edge_attr[rest0 + REST_P * TILES:E, :].rearrange("(a j) d -> a (j d)", a=1)

        def index_rows(a):
            return a[0:FULL * GROUP].rearrange("(g e) -> g e", e=GROUP), \
                a[FULL * GROUP:E].rearrange("(a e) -> a e", a=1)

        def column(a):
            return a.rearrange("(p a) -> p a", a=1)

        block = ctx.enter_context(nc.Block())

        @block.sync
        def _(sp):
            sp.wait_ge(rows_padded, 2)
            for rows, a, loaded in ((dst_rows, dst, dst_loaded), (src_rows, src, src_loaded)):
                full, rest = index_rows(a)
                sp.dma_start(rows[0:FULL, :], full).then_inc(loaded, 16)
                sp.dma_start(rows[FULL:GROUPS, 0:REST], rest).then_inc(loaded, 16)

            def load(g, u, free):
                sp.wait_ge(slots_free, free)
                sp.dma_start(edges[:, u, :], edge_full[g, :, :]).then_inc(edge_loaded[u], 16)

            def one_pass(done):
                sp.wait_ge(slots_free, done + SLOTS)
                sp.sem_inc(pass_begun, 1)
                with sp.Fori(0, FULL // SLOTS) as it:
                    for u in range(SLOTS):
                        load(it * SLOTS + u, u, done + it * SLOTS + (u + 1))
                sp.wait_ge(slots_free, done + FULL + 1)
                sp.dma_start(edges[0:REST_P, 0, :], edge_rest).then_inc(tail_loaded, 16)
                sp.dma_start(edges[REST_P:REST_P + 1, 0, 0:REST_E * D], edge_last).then_inc(tail_loaded, 16)

            one_pass(0)
            sp.wait_ge(mode_ready, 1)
            many = sp.value_load(wide_i[0:1, 0:1], min_val=0, max_val=1)
            with sp.If(many > 0):
                with sp.Fori(1, PASSES) as w:
                    one_pass(w * GROUPS)

            def store(k):
                sp.wait_ge(out_ready, BLOCK * (k + 1))
                sp.dma_start(out_blocks[k, :, :, :], xs[:, bass.ds(k * BLOCK, BLOCK), :]).then_inc(out_stored, 16)

            out_blocks = out[0:BLOCKS * BLOCK * P, :].rearrange("(k t p) d -> k p t d", p=P, t=BLOCK)
            with sp.Fori(0, BLOCKS) as k:
                store(k)
            sp.wait_ge(out_ready, NT)
            sp.dma_start(out[(NT - 1) * P:N, :], xs[0:LAST, NT - 1, :]).then_inc(out_stored, 16)
            sp.wait_ge(out_stored, 16 * (BLOCKS + 1))

        @block.gpsimd
        def _(pool):
            pool.iota(iota_i[:, :], [[1, P]], base=0, channel_multiplier=0)
            pool.iota(prow_i[:, :], [[0, 1]], base=0, channel_multiplier=1)
            pool.memset(ones[:, :], 1.0).then_inc(consts_ready, 1)
            pool.sem_inc(slots_free, SLOTS)
            pool.sem_inc(sums_free, 2)

            def gather(u, count):
                pool.wait_ge(indices_ready, count)
                pool.sem_inc(gather_begun, 1)
                for j in range(TILES):
                    pool.indirect_dma_start(gathered[:, u, j * D:(j + 1) * D], None, x,
                                            bass.IndirectOffsetOnAxis(src_slot[:, u, j:j + 1], 0)
                                            ).then_inc(gather_done[u], 16)

            def one_pass(done):
                with pool.Fori(0, FULL // SLOTS) as it:
                    for u in range(SLOTS):
                        gather(u, done + it * SLOTS + (u + 1))
                gather(0, done + GROUPS)

            one_pass(0)
            pool.wait_ge(mode_ready, 1)
            many = pool.value_load(wide_i[0:1, 0:1], min_val=0, max_val=1)
            with pool.If(many > 0):
                with pool.Fori(1, PASSES) as w:
                    one_pass(w * GROUPS)

        @block.scalar
        def _(act):
            for k, a in enumerate((b2, ln_w, ln_b, gn_w, gn_b, gn_ms)):
                act.dma_start(par[:, k:k + 1], column(a)).then_inc(params_loaded, 16)
            act.dma_start(w1[:, :], W1).then_inc(weights_loaded, 16)
            act.dma_start(w2[:, :, :], W2.rearrange("(c p) d -> p c d", p=P)).then_inc(weights_loaded, 16)
            for c in range(HC):
                act.dma_start(b1c[:, c:c + 1], column(b1[c * P:(c + 1) * P])).then_inc(weights_loaded, 16)
            act.dma_start(xs[:, 0:NT - 1, :], x[0:(NT - 1) * P, :].rearrange("(t p) d -> p t d", p=P)
                          ).then_inc(x_loaded, 16)
            act.dma_start(xs[0:LAST, NT - 1, :], x[(NT - 1) * P:N, :]).then_inc(x_loaded, 16)

            def stage(g, u, count):
                act.wait_ge(slots_free, count)
                nc.scalar.copy(src_slot[:, u, :], src_cols[:, :, bass.ds(g, 1)].rearrange("p j a -> p (j a)")
                               ).then_inc(indices_ready, 1)

            def one_pass(done):
                act.wait_ge(slots_free, done + SLOTS)
                with act.Fori(0, FULL // SLOTS) as it:
                    for u in range(SLOTS):
                        stage(it * SLOTS + u, u, done + it * SLOTS + (u + 1))
                stage(FULL, 0, done + GROUPS)

            act.wait_ge(cols_ready, 2)
            one_pass(0)
            act.wait_ge(mode_ready, 1)
            many = act.value_load(wide_i[0:1, 0:1], min_val=0, max_val=1)
            with act.If(many > 0):
                with act.Fori(1, PASSES) as w:
                    one_pass(w * GROUPS)

            act.wait_ge(weights_loaded, 16 * (2 + HC))

            def relu(u, count):
                act.wait_ge(z_ready, count)
                for c in range(HC):
                    nc.scalar.activation(hidden[:, u, c, :], zps[u][:, c, 0:CHUNK], ACT.Relu,
                                         bias=b1c[:, c:c + 1]).then_inc(hidden_ready, 1)

            with act.Fori(0, CHUNKS // 2) as it:
                for u in range(2):
                    relu(u, it * 2 + (u + 1))
            relu(0, CHUNKS)

            for k, a in enumerate((st[:, 4:5], st[:, 9:10])):
                act.wait_ge(root_in, k + 1)
                nc.scalar.activation(a, a, ACT.Sqrt).then_inc(root_out, 1)

            act.wait_ge(affine_ready, 1)

            def activate(k, u, free, width):
                if free is not None:
                    act.wait_ge(out_turned, free)
                nc.scalar.activation(gelu[:, u, 0:width], h[:, bass.ds(k * (BLOCK * P), width)],
                                     ACT.Gelu_apprx_tanh, scale=st[:, 10:11], bias=st[:, 12:13]
                                     ).then_inc(act_ready, 1)

            activate(0, 0, None, BLOCK * P)
            activate(1, 1, None, BLOCK * P)
            with act.Fori(1, BLOCKS // 2) as it:
                for u in range(2):
                    activate(it * 2 + u, u, it * 2 + (u - 1), BLOCK * P)
            activate(BLOCKS, 0, BLOCKS - 1, LAST)
            act.wait_ge(root_in, 3)
            nc.scalar.activation(rstd[:, :], rstd[:, :], ACT.Sqrt).then_inc(root_out, 1)

        @block.tensor
        def _(pe):
            pe.wait_ge(consts_ready, 2)
            pe.wait_ge(diag_ready, 1)
            for k in range(2):
                last = nc.tensor.matmul(hps[0][:, k * P:(k + 1) * P], ones[:, :], diag[:, k, :],
                                        start=(k == 0), stop=(k == 1), skip_group_check=True)
            last.then_inc(base_summed, 1)
            for k in range(2):
                pe.wait_ge(rows_ready, k + 1)
                for q in range(TILES // 4):
                    n = k * (TILES // 4) + q
                    if n >= 2:
                        pe.wait_ge(turned_free, n - 1)
                    for j in range(4):
                        rows = rows_f[:, k, :].rearrange("g (p j) -> g p j", j=TILES)
                        last = nc.tensor.transpose(tps[n % 2][:, j * P:(j + 1) * P], rows[:, :, q * 4 + j],
                                                   ident[:, :])
                    last.then_inc(turned, 1)

            def sum_group(u, s, count, uses, edge_sem, edge_count):
                pe.wait_ge(onehot_ready, count)
                pe.wait_ge(sums_free, count)
                pe.wait_ge(edge_sem, edge_count)
                oh = onehot[:, s, :].rearrange("p (j w) -> p j w", w=WINDOW)
                for k, data in enumerate((edges, gathered)):
                    if k:
                        pe.wait_ge(gather_done[u], uses * (16 * TILES))
                    for j in range(TILES):
                        last = nc.tensor.matmul(sums[s][:, 0:WINDOW], data[:, u, j * D:(j + 1) * D], oh[:, j, :],
                                                start=(k == 0 and j == 0), stop=(k == 1 and j == TILES - 1))
                last.then_inc(slots_free, 1)

            def one_pass(w):
                n = FULL // SLOTS
                with pe.Fori(0, n) as it:
                    for u in range(SLOTS):
                        uses = it + w * (n + 1 if u == 0 else n) + 1
                        sum_group(u, u % 2, w * GROUPS + it * SLOTS + (u + 1), uses, edge_loaded[u],
                                  (it + w * n + 1) * 16)
                sum_group(0, 0, w * GROUPS + GROUPS, w * (n + 1) + (n + 1), tail_loaded, w * 32 + 32)

            one_pass(0)
            pe.wait_ge(mode_ready, 1)
            many = pe.value_load(wide_i[0:1, 0:1], min_val=0, max_val=1)
            with pe.If(many > 0):
                with pe.Fori(1, PASSES) as w:
                    one_pass(w)

            pe.wait_ge(agg_ready, 1)
            pe.wait_ge(weights_loaded, 16 * (2 + HC))

            def up(c, u, free):
                if free is not None:
                    pe.wait_ge(hidden_ready, free)
                for k in range(HC):
                    last = nc.tensor.matmul(zps[u][:, k, 0:CHUNK], w1[:, k * P:(k + 1) * P],
                                            agg[:, bass.ds(c * CHUNK, CHUNK)], start=True, stop=True,
                                            skip_group_check=True)
                last.then_inc(z_ready, 1)

            def down(u, count, free):
                pe.wait_ge(hidden_ready, count)
                if free is not None:
                    pe.wait_ge(h_ready, free)
                for k in range(HC):
                    last = nc.tensor.matmul(hps[u][:, 0:CHUNK], w2[:, k, :], hidden[:, u, k, :],
                                            start=(k == 0), stop=(k == HC - 1))
                last.then_inc(h_summed, 1)

            up(0, 0, None)
            up(1, 1, None)
            down(0, HC, None)
            up(2, 0, HC)
            down(1, 2 * HC, None)
            with pe.Fori(0, (CHUNKS - 3) // 2) as it:
                for u in range(2):
                    up(it * 2 + (u + 3), 1 - u, it * (2 * HC) + (u + 2) * HC)
                    down(u, it * (2 * HC) + (u + 3) * HC, it * 2 + (u + 1))
            down(0, CHUNKS * HC, CHUNKS - 2)

            for k in range(2):
                pe.wait_ge(mean_in, k + 1)
                nc.tensor.matmul(hps[1][:, 256 + k:257 + k], ones[:, :], st[:, k:k + 1],
                                 start=True, stop=True, skip_group_check=True).then_inc(mean_summed, 1)

            def turn(u, count, free):
                pe.wait_ge(act_ready, count)
                if free is not None:
                    pe.wait_ge(y_ready, free)
                for t in range(BLOCK):
                    last = nc.tensor.transpose(tps[u][:, t * P:(t + 1) * P], gelu[:, u, t * P:(t + 1) * P],
                                               ident[:, :])
                last.then_inc(out_turned, 1)

            turn(0, 1, None)
            turn(1, 2, None)
            with pe.Fori(1, BLOCKS // 2) as it:
                for u in range(2):
                    turn(u, it * 2 + (u + 1), it * 2 + (u - 1))
            pe.wait_ge(act_ready, BLOCKS + 1)
            pe.wait_ge(y_ready, BLOCKS - 1)
            nc.tensor.transpose(tps[0][0:LAST, 0:P], gelu[:, 0, 0:LAST], ident[:, :]).then_inc(out_turned, 1)

        @block.vector
        def _(dve):
            steps = [0]

            def link(ins, chain, count):
                count[0] += 1
                ins.then_inc(chain, 1)
                dve.wait_ge(chain, count[0])

            dve.memset(dst_rows[96:P, :], -1).then_inc(rows_padded, 1)
            dve.memset(src_rows[96:P, :], 0).then_inc(rows_padded, 1)
            dve.memset(agg[:, :], 0.0)
            dve.memset(lo[:, :], 0.0)
            link(dve.memset(hi[:, :], 0.0), setup, steps)
            dve.wait_ge(consts_ready, 1)
            dve.tensor_copy(iota_f[:, :], iota_i[:, :])
            link(dve.tensor_copy(prow_f[:, :], prow_i[:, :]), setup, steps)
            dve.tensor_scalar(ident[:, :], iota_f[:, :], prow_f[:, 0:1], None, ALU.is_equal
                              ).then_inc(consts_ready, 1)

            link(dve.memset(rows_f[96:P, :, :], 0.0), setup, steps)
            dve.wait_ge(dst_loaded, 32)
            link(dve.tensor_copy(rows_f[0:GROUPS, 0, :], dst_rows[0:GROUPS, :]), setup, steps)
            dve.tensor_reduce(hi[0:GROUPS, :], rows_f[0:GROUPS, 0, :], AX_X, ALU.max)
            link(dve.tensor_scalar(pad_f[0:GROUPS, :], rows_f[0:GROUPS, 0, REST:GROUP], 0.0, PAD,
                                   ALU.is_lt, ALU.mult), setup, steps)
            link(dve.tensor_tensor(rows_f[0:GROUPS, 0, REST:GROUP], rows_f[0:GROUPS, 0, REST:GROUP],
                                   pad_f[0:GROUPS, :], ALU.add), setup, steps)
            dve.engine_nop().then_inc(rows_ready, 1)
            link(dve.tensor_reduce(lo[0:GROUPS, :], rows_f[0:GROUPS, 0, :], AX_X, ALU.min), setup, steps)
            link(dve.tensor_tensor(hi[:, :], hi[:, :], lo[:, :], ALU.subtract), setup, steps)
            dve.tensor_scalar(diag[:, 0, :], ident[:, :], lo[:, 0:1], None, ALU.mult)
            dve.tensor_scalar(diag[:, 1, :], ident[:, :], hi[:, 0:1], None, ALU.mult).then_inc(diag_ready, 1)
            dve.wait_ge(src_loaded, 32)
            dve.tensor_copy(rows_f[0:GROUPS, 1, :], src_rows[0:GROUPS, :]).then_inc(rows_ready, 1)

            dve.wait_ge(base_summed, 1)
            link(dve.tensor_reduce(wide[:, :], hps[0][:, P:2 * P], AX_X, ALU.max), setup, steps)
            link(dve.tensor_scalar(wide[:, :], wide[:, :], float(WINDOW), None, ALU.is_ge), setup, steps)
            dve.tensor_copy(wide_i[:, :], wide[0:1, :]).then_inc(mode_ready, 1)
            link(dve.tensor_scalar(narrow[:, :], wide[:, :], -1.0, 1.0, ALU.mult, ALU.add), setup, steps)
            link(dve.tensor_scalar(base_f[:, :], hps[0][:, 0:P], narrow[:, 0:1], None, ALU.mult), setup, steps)
            link(dve.tensor_copy(base_i[:, :], base_f[0:1, :]), setup, steps)

            for k in range(2):
                for q in range(TILES // 4):
                    n = k * (TILES // 4) + q
                    dve.wait_ge(turned, n + 1)
                    got = tps[n % 2][:, :].rearrange("p (j g) -> p j g", g=P)
                    if k == 0:
                        step = dve.tensor_tensor(dst_cols[:, q * 4:q * 4 + 4, :], got,
                                                 base_f[:, :].rearrange("p (a g) -> p a g", a=1).to_broadcast([P, 4, P]),
                                                 ALU.subtract)
                    else:
                        step = dve.tensor_copy(src_cols[:, q * 4:q * 4 + 4, :], got)
                    step.then_inc(turned_free, 1)
                dve.wait_ge(turned_free, (k + 1) * (TILES // 4))
                dve.engine_nop().then_inc(cols_ready, 1)

            window = iota_f[:, 0:WINDOW].rearrange("p (a w) -> p a w", a=1).to_broadcast([P, TILES, WINDOW])

            def mark(g, s, count):
                dve.wait_ge(slots_free, count)
                oh = onehot[:, s, :].rearrange("p (j w) -> p j w", w=WINDOW)
                dve.tensor_tensor(oh, window, dst_cols[:, :, bass.ds(g, 1)].to_broadcast([P, TILES, WINDOW]),
                                  ALU.is_equal).then_inc(onehot_ready, 1)

            def add(g, s, count):
                base = dve.value_load(base_i[0:1, bass.ds(g, 1)], min_val=0, max_val=N - 1)
                dve.wait_ge(slots_free, count + SLOTS)
                dve.wait_ge(sums_free, count + 1)
                at = agg[:, bass.ds(base, WINDOW)]
                dve.tensor_tensor(at, at, sums[s][:, 0:WINDOW], ALU.add).then_inc(sums_free, 1)

            def one_pass(done):
                mark(0, 0, done + SLOTS)
                with dve.Fori(0, FULL // 2) as it:
                    for s in range(2):
                        g = it * 2 + s
                        mark(g + 1, 1 - s, done + g + (SLOTS))
                        add(g, s, done + g + 1)
                add(FULL, FULL % 2, done + GROUPS)
                dve.wait_ge(sums_free, done + GROUPS + 2)

            one_pass(0)
            many = dve.value_load(wide_i[0:1, 0:1], min_val=0, max_val=1)
            with dve.If(many > 0):
                with dve.Fori(1, PASSES) as w:
                    dve.tensor_scalar(dst_cols[:, :, :], dst_cols[:, :, :], -float(WINDOW), None, ALU.add
                                      ).then_inc(shifted, 1)
                    dve.tensor_scalar(base_f[:, :], base_f[:, :], float(WINDOW), None, ALU.add).then_inc(shifted, 1)
                    dve.wait_ge(shifted, w * 3 - 1)
                    dve.tensor_copy(base_i[:, :], base_f[0:1, :]).then_inc(shifted, 1)
                    dve.wait_ge(shifted, w * 3)
                    one_pass(w * GROUPS)
            dve.engine_nop().then_inc(agg_ready, 1)

            dve.wait_ge(params_loaded, 16 * 6)

            def keep(c, u, count):
                hc = h[:, bass.ds(c * CHUNK, CHUNK)]
                dve.wait_ge(h_summed, count)
                dve.tensor_scalar(hc, hps[u][:, 0:CHUNK], par[:, B2:B2 + 1], None, ALU.add).then_inc(h_ready, 1)
                dve.wait_ge(h_ready, count)
                dve.bn_stats(stats[:, bass.ds(c, 1), :].rearrange("p a s -> p (a s)"), hc).then_inc(h_stats, 1)

            with dve.Fori(0, CHUNKS // 2) as it:
                for u in range(2):
                    keep(it * 2 + u, u, it * 2 + (u + 1))
            keep(CHUNKS - 1, 0, CHUNKS)
            dve.wait_ge(h_stats, CHUNKS)

            steps = [0]

            def step(ins):
                link(ins, norm, steps)

            def c(k):
                return st[:, k:k + 1]

            m, v = mv[:, 0:1], mv[:, 1:2]
            step(dve.bn_aggr(mv[:, :], stats[:, :, :].rearrange("p c s -> p (c s)")))
            dve.tensor_scalar(c(0), m, 1.0 / D, None, ALU.mult).then_inc(mean_in, 1)
            dve.wait_ge(mean_summed, 1)
            step(dve.tensor_tensor(c(2), m, hps[1][:, 256:257], ALU.subtract))
            step(dve.tensor_tensor(c(3), c(2), c(2), ALU.mult))
            step(dve.tensor_tensor(c(3), c(3), v, ALU.add))
            dve.tensor_scalar(c(1), c(3), 1.0 / D, None, ALU.mult).then_inc(mean_in, 1)
            dve.wait_ge(mean_summed, 2)
            dve.tensor_scalar(c(4), hps[1][:, 257:258], EPS, None, ALU.add).then_inc(root_in, 1)
            dve.wait_ge(root_out, 1)
            step(dve.reciprocal(c(4), c(4)))
            step(dve.tensor_tensor(c(5), c(4), par[:, LNW:LNW + 1], ALU.mult))
            step(dve.tensor_scalar(c(6), c(2), c(5), par[:, LNB:LNB + 1], ALU.mult, ALU.add))
            step(dve.tensor_tensor(c(7), c(6), par[:, GNM:GNM + 1], ALU.mult))
            step(dve.tensor_tensor(c(7), c(6), c(7), ALU.subtract))
            step(dve.tensor_tensor(c(8), c(7), c(7), ALU.mult))
            step(dve.tensor_tensor(c(9), c(5), c(5), ALU.mult))
            step(dve.scalar_tensor_tensor(c(9), v, c(9), c(8), ALU.mult, ALU.add))
            dve.tensor_scalar(c(9), c(9), EPS, None, ALU.add).then_inc(root_in, 1)
            dve.wait_ge(root_out, 2)
            step(dve.reciprocal(c(9), c(9)))
            step(dve.tensor_tensor(c(9), c(9), par[:, GNW:GNW + 1], ALU.mult))
            step(dve.tensor_tensor(c(10), c(5), c(9), ALU.mult))
            step(dve.tensor_scalar(c(11), c(7), c(9), par[:, GNB:GNB + 1], ALU.mult, ALU.add))
            step(dve.tensor_tensor(c(12), c(10), m, ALU.mult))
            step(dve.tensor_tensor(c(12), c(11), c(12), ALU.subtract))
            dve.engine_nop().then_inc(affine_ready, 1)

            dve.wait_ge(x_loaded, 32)

            def finish(t0, u, count, tiles, rows):
                y = xs[0:rows, bass.ds(t0, tiles), :]
                dve.wait_ge(out_turned, count)
                got = tps[u][0:rows, 0:tiles * P].rearrange("p (t d) -> p t d", d=P)
                dve.scalar_tensor_tensor(y, y, 2.0, got, ALU.mult, ALU.add).then_inc(y_ready, 1)
                dve.wait_ge(y_ready, count)
                for t in range(tiles):
                    dve.bn_stats(lnstats[0:rows, bass.ds(t0 + t, 1), :].rearrange("p a s -> p (a s)"),
                                 xs[0:rows, bass.ds(t0 + t, 1), :].rearrange("p a d -> p (a d)")
                                 ).then_inc(ln_stats, 1)

            dve.memset(lnstats[:, NT - 1, :], 1.0).then_inc(ln, 1)
            dve.wait_ge(ln, 1)
            with dve.Fori(0, BLOCKS // 2) as it:
                for u in range(2):
                    finish(it * (2 * BLOCK) + u * BLOCK, u, it * 2 + (u + 1), BLOCK, P)
            finish(NT - 1, 0, BLOCKS + 1, 1, LAST)
            dve.wait_ge(ln_stats, NT)

            steps = [1]

            def lnstep(ins):
                link(ins, ln, steps)

            even, odd = lnstats[:, :, 1], lnstats[:, :, 4]
            dve.tensor_tensor(lngap[:, :], even, odd, ALU.subtract)
            lnstep(dve.tensor_tensor(lnmean[:, :], even, odd, ALU.add))
            dve.tensor_scalar(lnmean[:, :], lnmean[:, :], 0.5, None, ALU.mult)
            dve.tensor_tensor(rstd[:, :], lnstats[:, :, 2], lnstats[:, :, 5], ALU.add)
            lnstep(dve.tensor_tensor(lngap[:, :], lngap[:, :], lngap[:, :], ALU.mult))
            dve.tensor_scalar(lngap[:, :], lngap[:, :], 0.25, EPS, ALU.mult, ALU.add)
            lnstep(dve.tensor_scalar(rstd[:, :], rstd[:, :], 1.0 / D, None, ALU.mult))
            dve.tensor_tensor(rstd[:, :], rstd[:, :], lngap[:, :], ALU.add).then_inc(root_in, 1)
            dve.wait_ge(root_out, 3)
            lnstep(dve.reciprocal(rstd[:, :], rstd[:, :]))

            def normalise(t, rows):
                yt = xs[0:rows, bass.ds(t, 1), :].rearrange("p a d -> p (a d)")
                dve.tensor_scalar(yt, yt, lnmean[0:rows, bass.ds(t, 1)], rstd[0:rows, bass.ds(t, 1)],
                                  ALU.subtract, ALU.mult).then_inc(out_ready, 1)

            with dve.Fori(0, BLOCKS) as k:
                for t in range(BLOCK):
                    normalise(k * BLOCK + t, P)
            normalise(NT - 1, LAST)


_INS = ['x', 'src', 'dst', 'edge_attr_128', 'L0_gnn_W1', 'L0_gnn_b1', 'L0_gnn_W2', 'L0_gnn_b2', 'L0_gnn_ln_w',
        'L0_gnn_ln_b', 'L0_gnn_gn_w', 'L0_gnn_gn_b', 'L0_gnn_gn_ms']
_OUTS = [((6250, 128), 'float32')]


def kernel(**inputs):
    import numpy as _np
    import concourse.bacc as _bacc
    from concourse import mybir as _mybir
    from concourse.bass_utils import run_bass_kernel_spmd as _run

    nc = _bacc.Bacc("TRN2", target_bir_lowering=False, num_devices=1)
    arrays, args = {}, []
    for name in _INS:
        a = _np.ascontiguousarray(inputs[name])
        arrays[f"in_{name}_dram"] = a
        args.append(nc.dram_tensor(f"in_{name}_dram", a.shape, _mybir.dt.from_np(a.dtype), kind="ExternalInput").ap())
    for i, (shape, dtype) in enumerate(_OUTS):
        dt = _mybir.dt.from_np(_np.dtype(dtype))
        args.append(nc.dram_tensor(f"out_{i}_dram", shape, dt, kind="ExternalOutput").ap())
    gnn_kernel(nc, *args)
    r = _run(nc, [arrays], core_ids=[0])
    got = tuple(r.results[0][f"out_{i}_dram"] for i in range(len(_OUTS)))
    return got[0]
```

```python
from contextlib import ExitStack

import concourse.bass as bass
from concourse import mybir

ALU = mybir.AluOpType
ACT = mybir.ActivationFunctionType
F32 = mybir.dt.float32
F32R = mybir.dt.float32r
BF16 = mybir.dt.bfloat16
I32 = mybir.dt.int32
I16 = mybir.dt.int16
AX_X = mybir.AxisListType.X

P = 128
EPS = 1e-5

TILES = 16
GROUP = P * TILES
WINDOW = 80
HALF = TILES // 2
HALVES = 6
GPC = 3
HPC = 2 * GPC
PAD = 1.0e6

PAIR = 2
STRIDE = 16
CHUNK = 250
PAIRS = CHUNK // PAIR
BATCH = 25
BATCHES = PAIRS // BATCH
BP = BATCH + 1
BANK = 5
BANKS = PAIRS // BANK
BPB = BATCH // BANK
RING = 3
SHIFT = 7

BLOCK = 4


def gnn_kernel(nc, x, src, dst, edge_attr, W1, b1, W2, b2, ln_w, ln_b, gn_w, gn_b, gn_ms, out):
    N, D = x.shape
    E = src.shape[0]
    H = W1.shape[1]
    HC = H // P
    FULL = E // GROUP
    REST = E - FULL * GROUP
    REST_P, REST_E = REST // TILES, REST % TILES
    GROUPS = FULL + 1
    CHUNKS = N // CHUNK
    LEAD = (FULL // GPC) - CHUNKS
    LEAD0 = 2
    assert D == P and REST and REST_E > HALF and GROUPS <= P and FULL == (LEAD + CHUNKS) * GPC + 1
    assert CHUNKS * CHUNK == N and CHUNKS % 2 == 1 and LEAD > LEAD0 + 3
    PASSES = -(-N // WINDOW)
    NT = -(-N // P)
    LAST = N - (NT - 1) * P
    BLOCKS = (NT - 1) // BLOCK
    assert BLOCKS * BLOCK == NT - 1 and BLOCKS % 2 == 0
    KEYS = PAIR * NT
    ET = E // P
    SETS = -(-ET // P)
    NPAIR = N // PAIR
    ROWS = ET * (P // STRIDE) + 1
    SAFE = (E - P) // STRIDE // 16 * 16
    LATE = ROWS - SAFE
    LATE_E = E - SAFE * STRIDE
    LATE_W = (LATE - 1) * STRIDE + P

    rows_dst = nc.dram_tensor("rows_dst", (ROWS, P), I32, kind="Internal").ap()
    rows_src = nc.dram_tensor("rows_src", (ROWS, P), I32, kind="Internal").ap()

    with ExitStack() as ctx:
        def sb(name, shape, dt=F32):
            return ctx.enter_context(nc.sbuf_tensor(name, shape, dt))

        def psum(name, shape, dt=F32):
            return ctx.enter_context(nc.psum_tensor(name, shape, dt))

        def sem(name):
            return ctx.enter_context(nc.semaphore(name))

        pool_e = sb("pool_e", [P, NT * D])
        edges = pool_e[:, 0:HALVES * HALF * D].rearrange("p (u e) -> p u e", u=HALVES)
        xs = pool_e[:, :].rearrange("p (t d) -> p t d", d=D)
        onehot = sb("onehot", [P, 2, HALF * WINDOW])
        counts = sb("counts", [P, NT, CHUNK], F32R)
        x_hi = sb("x_hi", [P, NT, D], F32R)
        x_lo = sb("x_lo", [P, NT, D], F32R)
        LW = P * BP
        KW = KEYS * BP
        pool_m = sb("pool_m", [P, 2 * NT * D], BF16)
        mark_lo = [pool_m[:, s * (LW + KW):s * (LW + KW) + LW].rearrange("p (v n) -> p v n", n=BP) for s in range(2)]
        mark_key = [pool_m[:, s * (LW + KW) + LW:(s + 1) * (LW + KW)].rearrange("p (v n) -> p v n", n=BP)
                    for s in range(2)]
        x_raw = pool_m[:, :].bitcast(F32)
        below = pool_m[:, 0:2 * NPAIR + 14].rearrange("p (s v) -> p s v", s=2)
        pair_row = pool_m[:, 2 * NPAIR + 14:3 * NPAIR + 21].bitcast(I16)
        values = sb("values", [P, P, BP], BF16)
        agg = sb("agg", [P, N + WINDOW])
        h = agg[:, 0:N]
        rows_f = agg[:, 0:GROUP]
        rows_i = agg[:, GROUP:2 * GROUP].bitcast(I32)
        pad_f = agg[:, 2 * GROUP:3 * GROUP - REST]
        dst_cols = sb("dst_cols", [P, TILES, GROUPS])
        late = sb("late", [1, 2, LATE_W], I32)
        hidden = onehot[:, :, :].rearrange("p s e -> p (s e)")[:, 0:2 * HC * CHUNK].rearrange(
            "p (u k n) -> p u k n", u=2, k=HC)
        gelu = dst_cols[:, :, :].rearrange("p j g -> p (j g)")[:, 0:2 * BLOCK * P].rearrange("p (u n) -> p u n", u=2)
        w1 = sb("w1", [P, H])
        w2 = sb("w2", [P, HC, D])
        b1c = sb("b1c", [P, HC])
        par = sb("par", [P, 6])
        B2, LNW, LNB, GNW, GNB, GNM = range(6)
        iota_i = sb("iota_i", [P, P], I32)
        iota_f = sb("iota_f", [P, P])
        prow_i = sb("prow_i", [P, 1], I32)
        prow_f = sb("prow_f", [P, 1])
        pair_i = sb("pair_i", [P, CHUNKS + 1], I32)
        pair_f = sb("pair_f", [P, CHUNKS + 1])
        tile_end_i = sb("tile_end_i", [P, SETS], I32)
        tile_end = sb("tile_end", [P, SETS])
        tile_f = sb("tile_f", [P, CHUNKS + 1])
        tile_slot = sb("tile_slot", [P, 1], I32)
        row_slot = sb("row_slot", [P, 1], I32)
        first_i = sb("first_i", [P, 1], I32)
        first_f = sb("first_f", [P, 1])
        begins = sb("begins", [P, P], I32)
        junk = sb("junk", [P, P])
        near = sb("near", [P, 2, P], I32)
        lo_i = sb("lo_i", [P, P], I32)
        hi_i = sb("hi_i", [P, P], I32)
        lo_f = sb("lo_f", [P, P])
        node_f = sb("node_f", [P, P])
        covered = sb("covered", [P, CHUNKS + 1])
        turned_lo = sb("turned_lo", [P, BATCHES, BP], BF16)
        turned_key = sb("turned_key", [P, BATCHES, BP], BF16)
        ident = sb("ident", [P, P])
        ones = sb("ones", [P, P])
        ones_b = sb("ones_b", [P, 1], BF16)
        lo = sb("lo", [P, 1])
        hi = sb("hi", [P, 1])
        base_f = sb("base_f", [P, P])
        base_i = sb("base_i", [1, P], I32)
        wide = sb("wide", [P, 2])
        flag_i = sb("flag_i", [1, 1], I32)
        sums = sb("sums", [P, 3, D])
        diag = sums[:, 0:2, :]
        edge_dst = sb("edge_dst", [P, TILES], I32)
        edge_src = sb("edge_src", [P, TILES], I32)
        edge_dst_f = sb("edge_dst_f", [P, TILES])
        pass_base = sb("pass_base", [P, 1])
        stats = sb("stats", [P, CHUNKS, 6])
        mv = sb("mv", [P, 2])
        st = sb("st", [P, 24])
        lnstats = sb("lnstats", [P, NT, 6])
        lnmean = sb("lnmean", [P, NT])
        lngap = sb("lngap", [P, NT])
        rstd = sb("rstd", [P, NT])

        banks = [psum(f"bank{i}", [P, 512]) for i in range(8)]
        cps = banks[0:RING]
        eps = [b[0:WINDOW, 0:D] for b in banks[3:6]]
        turned_sum = [b[:, D:D + WINDOW] for b in banks[3:6]]
        turn_ps, sps = banks[6], banks[7]
        KEY0, LO0 = 0, P
        zps = [banks[u][:, :].rearrange("p (k n) -> p k n", k=HC) for u in range(2)]
        hps = [banks[2], banks[3]]
        ops = [banks[4], sps]

        rows_padded = sem("rows_padded")
        dst_loaded = sem("dst_loaded")
        ends_loaded = sem("ends_loaded")
        late_loaded = sem("late_loaded")
        table_built = sem("table_built")
        x_loaded = sem("x_loaded")
        x_split = sem("x_split")
        x_high = sem("x_high")
        consts_ready = sem("consts_ready")
        setup = sem("setup")
        diag_ready = sem("diag_ready")
        base_summed = sem("base_summed")
        rows_ready = sem("rows_ready")
        turned = sem("turned")
        below_ready = sem("below_ready")
        below_used = sem("below_used")
        tiles_found = sem("tiles_found")
        edge_loaded = [sem(f"edge_loaded{i}") for i in range(HALVES)]
        tail_loaded = sem("tail_loaded")
        onehot_ready = sem("onehot_ready")
        halves_free = sem("halves_free")
        sums_copied = sem("sums_copied")
        sums_turned = sem("sums_turned")
        edges_added = sem("edges_added")
        tile_staged = sem("tile_staged")
        row_staged = sem("row_staged")
        gathers_begun = sem("gathers_begun")
        begins_loaded = sem("begins_loaded")
        near_loaded = sem("near_loaded")
        prep = sem("prep")
        keys_made = sem("keys_made")
        keys_turned = sem("keys_turned")
        keys_ready = sem("keys_ready")
        pads_ready = sem("pads_ready")
        marks_ready = sem("marks_ready")
        banks_done = sem("banks_done")
        banks_free = sem("banks_free")
        chunk_summed = sem("chunk_summed")
        chunk_added = sem("chunk_added")
        cover_in = sem("cover_in")
        cover_summed = sem("cover_summed")
        mode_ready = sem("mode_ready")
        agg_clear = sem("agg_clear")
        slots_clear = sem("slots_clear")
        group_loaded = sem("group_loaded")
        group_gathered = sem("group_gathered")
        group_marked = sem("group_marked")
        group_summed = sem("group_summed")
        group_copied = sem("group_copied")
        group_turned = sem("group_turned")
        group_added = sem("group_added")
        gchain = sem("gchain")
        passes_begun = sem("passes_begun")
        agg_ready = sem("agg_ready")
        weights_loaded = sem("weights_loaded")
        params_loaded = sem("params_loaded")
        xs_loaded = sem("xs_loaded")
        z_ready = sem("z_ready")
        hidden_ready = sem("hidden_ready")
        h_summed = sem("h_summed")
        h_ready = sem("h_ready")
        h_stats = sem("h_stats")
        norm = sem("norm")
        mean_in = sem("mean_in")
        mean_summed = sem("mean_summed")
        affine_ready = sem("affine_ready")
        act_ready = sem("act_ready")
        out_turned = sem("out_turned")
        y_ready = sem("y_ready")
        ln_stats = sem("ln_stats")
        ln = sem("ln")
        root_in = sem("root_in")
        root_out = sem("root_out")
        out_ready = sem("out_ready")
        out_stored = sem("out_stored")

        HD = HALF * D
        edge_full = edge_attr[0:FULL * GROUP, :].rearrange("(g p j) d -> g p (j d)", p=P, j=TILES)
        rest0 = FULL * GROUP
        edge_rest = edge_attr[rest0:rest0 + REST_P * TILES, :].rearrange("(p j) d -> p (j d)", j=TILES)
        edge_last = edge_attr[rest0 + REST_P * TILES:E, :].rearrange("(a j) d -> a (j d)", a=1)
        dst_full = dst[0:FULL * GROUP].rearrange("(g e) -> g e", e=GROUP)
        dst_rest = dst[FULL * GROUP:E].rearrange("(a e) -> a e", a=1)
        dst_tiles = dst[0:ET * P].rearrange("(t e) -> t e", e=P)

        def column(a):
            return a.rearrange("(p a) -> p a", a=1)

        def load_rest(eng, u0, loaded):
            for k in range(2):
                more = min(HALF, REST_E - k * HALF) * D
                eng.dma_start(edges[0:REST_P, u0 + k, :], edge_rest[:, k * HD:(k + 1) * HD]).then_inc(loaded, 16)
                eng.dma_start(edges[REST_P:REST_P + 1, u0 + k, 0:more],
                              edge_last[:, k * HD:k * HD + more]).then_inc(loaded, 16)

        block = ctx.enter_context(nc.Block())

        @block.sync
        def _(sp):
            sp.wait_ge(rows_padded, 1)
            sp.dma_start(rows_i[0:FULL, :], dst_full).then_inc(dst_loaded, 16)
            sp.dma_start(rows_i[FULL:GROUPS, 0:REST], dst_rest).then_inc(dst_loaded, 16)

            def load(g, k, u, free):
                sp.wait_ge(halves_free, free)
                sp.dma_start(edges[:, u, :], edge_full[g, :, k * HD:(k + 1) * HD]).then_inc(edge_loaded[u], 16)

            with sp.Fori(0, LEAD + CHUNKS) as r:
                for u in range(HPC):
                    load(r * GPC + u // 2, u % 2, u, r * HPC + (u + 1))
            for k in range(2):
                load(FULL - 1, k, k, 2 * (FULL - 1) + k + 1)
            sp.wait_ge(halves_free, 2 * FULL + 2)
            load_rest(sp, 2, tail_loaded)

            def general(n):
                sp.wait_ge(slots_clear, n + 1)
                sp.sem_inc(passes_begun, 1)

            def load_group(g, n):
                general(n)
                for k in range(2):
                    sp.dma_start(edges[:, k, :], edge_full[g, :, k * HD:(k + 1) * HD]).then_inc(group_loaded, 16)
                for to, a in ((edge_dst, dst), (edge_src, src)):
                    v = a[0:FULL * GROUP].rearrange("(g p j) -> g p j", p=P, j=TILES)
                    sp.dma_start(to[:, :], v[g, :, :]).then_inc(group_loaded, 16)
                for _ in range(4):
                    sp.sem_inc(group_loaded, 16)

            sp.wait_ge(mode_ready, 1)
            with sp.If(sp.value_load(flag_i[0:1, 0:1], min_val=0, max_val=1) > 0):
                with sp.Fori(0, PASSES) as w:
                    with sp.Fori(0, FULL) as g:
                        load_group(g, w * GROUPS + g)
                    general(w * GROUPS + FULL)
                    load_rest(sp, 0, group_loaded)
                    for to, a in ((edge_dst, dst), (edge_src, src)):
                        whole = a[rest0:rest0 + REST_P * TILES].rearrange("(p j) -> p j", j=TILES)
                        more = a[rest0 + REST_P * TILES:E].rearrange("(a j) -> a j", a=1)
                        sp.dma_start(to[0:REST_P, :], whole).then_inc(group_loaded, 16)
                        sp.dma_start(to[REST_P:REST_P + 1, 0:REST_E], more).then_inc(group_loaded, 16)

            sp.wait_ge(agg_ready, 1)
            sp.dma_start(xs[:, 0:NT - 1, :], x[0:(NT - 1) * P, :].rearrange("(t p) d -> p t d", p=P)
                         ).then_inc(xs_loaded, 16)
            sp.dma_start(xs[0:LAST, NT - 1, :], x[(NT - 1) * P:N, :]).then_inc(xs_loaded, 16)

            out_blocks = out[0:BLOCKS * BLOCK * P, :].rearrange("(k t p) d -> k p t d", p=P, t=BLOCK)
            with sp.Fori(0, BLOCKS) as k:
                sp.wait_ge(out_ready, BLOCK * (k + 1))
                sp.dma_start(out_blocks[k, :, :, :], xs[:, bass.ds(k * BLOCK, BLOCK), :]).then_inc(out_stored, 16)
            sp.wait_ge(out_ready, NT)
            sp.dma_start(out[(NT - 1) * P:N, :], xs[0:LAST, NT - 1, :]).then_inc(out_stored, 16)
            sp.wait_ge(out_stored, 16 * (BLOCKS + 1))

        @block.gpsimd
        def _(pool):
            pool.iota(iota_i[:, :], [[1, P]], base=0, channel_multiplier=0)
            pool.iota(prow_i[:, :], [[0, 1]], base=0, channel_multiplier=1)
            pool.iota(pair_i[:, :], [[PAIR * PAIRS, CHUNKS + 1]], base=0, channel_multiplier=PAIR)
            pool.memset(ones_b[:, :], 1.0)
            pool.memset(ones[:, :], 1.0).then_inc(consts_ready, 1)
            for s, places in ((halves_free, HALVES), (sums_copied, 3), (sums_turned, 3), (edges_added, 3),
                              (banks_done, 1), (chunk_summed, 1), (chunk_added, 1)):
                pool.sem_inc(s, places)
            pool.wait_ge(x_split, 2)
            pool.iota(pair_row, [[1, NPAIR + 7]], base=0, channel_multiplier=0,
                      allow_small_or_imprecise_dtypes=True).then_inc(consts_ready, 1)

            def offset(slot):
                return bass.IndirectOffsetOnAxis(slot[0:PAIRS, 0:1], 0)

            pool.wait_ge(table_built, 64)
            with pool.Fori(0, CHUNKS + 1) as c:
                pool.wait_ge(tile_staged, c + 1)
                pool.sem_inc(gathers_begun, 1)
                pool.indirect_dma_start(begins[0:PAIRS, :], None, dst_tiles, offset(tile_slot)
                                        ).then_inc(begins_loaded, 16)
                pool.wait_ge(row_staged, c + 1)
                pool.sem_inc(gathers_begun, 1)
                for k, rows in enumerate((rows_src, rows_dst)):
                    pool.indirect_dma_start(near[0:PAIRS, k, :], None, rows, offset(row_slot)
                                            ).then_inc(near_loaded, 16)

            pool.wait_ge(mode_ready, 1)
            with pool.If(pool.value_load(flag_i[0:1, 0:1], min_val=0, max_val=1) > 0):
                with pool.Fori(0, PASSES * GROUPS) as n:
                    pool.wait_ge(group_loaded, (n + 1) * 128)
                    pool.sem_inc(gathers_begun, 1)
                    for j in range(TILES):
                        pool.indirect_dma_start(edges[:, 2 + j // HALF, (j % HALF) * D:(j % HALF + 1) * D], None, x,
                                                bass.IndirectOffsetOnAxis(edge_src[:, j:j + 1], 0)
                                                ).then_inc(group_gathered, 16)

        @block.scalar
        def _(act):
            act.dma_start(x_raw[:, 0:(NT - 1) * D].rearrange("p (t d) -> p t d", d=D),
                          x[0:(NT - 1) * P, :].rearrange("(t p) d -> p t d", p=P)).then_inc(x_loaded, 16)
            act.wait_ge(rows_padded, 3)
            act.dma_start(x_raw[0:LAST, (NT - 1) * D:NT * D], x[(NT - 1) * P:N, :]).then_inc(x_loaded, 16)
            whole = (SETS - 1) * P
            with nc.allow_non_contiguous_dma("a word of each tile"):
                act.dma_start(tile_end_i[:, 0:SETS - 1],
                              dst_tiles[0:whole, P - 1].rearrange("(s p) -> p s", p=P)).then_inc(ends_loaded, 16)
                act.dma_start(tile_end_i[0:ET - whole, SETS - 1:SETS],
                              dst_tiles[whole:ET, P - 1:P]).then_inc(ends_loaded, 16)
            for k, a in enumerate((src, dst)):
                act.dma_start(late[0:1, k, 0:LATE_E], a[SAFE * STRIDE:E].rearrange("(a e) -> a e", a=1)
                              ).then_inc(late_loaded, 16)
            act.wait_ge(late_loaded, 32)
            for k, (a, rows) in enumerate(((src, rows_src), (dst, rows_dst))):
                act.dma_start(rows[0:SAFE, :], bass.AP(a.tensor, 0, [[STRIDE, SAFE], [1, P]])
                              ).then_inc(table_built, 16)
                v = late[0:1, k, :]
                act.dma_start(rows[SAFE:ROWS, :].rearrange("(a r) e -> a r e", a=1),
                              bass.AP(v.tensor, v.offset, [v.ap[0], [STRIDE, LATE], [1, P]])
                              ).then_inc(table_built, 16)
            for k, a in enumerate((b2, ln_w, ln_b, gn_w, gn_b, gn_ms)):
                act.dma_start(par[:, k:k + 1], column(a)).then_inc(params_loaded, 16)
            act.dma_start(w1[:, :], W1).then_inc(weights_loaded, 16)
            act.dma_start(w2[:, :, :], W2.rearrange("(c p) d -> p c d", p=P)).then_inc(weights_loaded, 16)
            for c in range(HC):
                act.dma_start(b1c[:, c:c + 1], column(b1[c * P:(c + 1) * P])).then_inc(weights_loaded, 16)
            act.wait_ge(x_loaded, 32)
            nc.scalar.copy(x_hi[:, :, :], x_raw.rearrange("p (t d) -> p t d", d=D)).then_inc(x_high, 1)

            def copy_sums(g, s):
                act.wait_ge(halves_free, g * 2 + (2 + HALVES))
                act.wait_ge(sums_turned, g + 1)
                nc.scalar.copy(sums[0:WINDOW, s, :], eps[s]).then_inc(sums_copied, 1)

            def three_copies(r):
                for j in range(GPC):
                    copy_sums(r * GPC + j, j)

            def copy_keys(c):
                act.wait_ge(marks_ready, c * BATCHES)
                act.wait_ge(keys_turned, c + 1)
                for at, to in ((LO0, turned_lo), (KEY0, turned_key)):
                    nc.scalar.copy(to[:, :, 0:BATCH], turn_ps[:, at:at + PAIRS].rearrange("p (b n) -> p b n", n=BATCH)
                                   ).then_inc(keys_ready, 1)

            for r in range(LEAD0):
                three_copies(r)
            with act.Fori(LEAD0, LEAD) as r:
                three_copies(r)
            act.wait_ge(pads_ready, 1)
            act.wait_ge(keys_turned, 1)
            for at, to in ((LO0, turned_lo), (KEY0, turned_key)):
                nc.scalar.copy(to[:, :, 0:BATCH], turn_ps[:, at:at + PAIRS].rearrange("p (b n) -> p b n", n=BATCH)
                               ).then_inc(keys_ready, 1)

            def copy_chunk(c):
                act.wait_ge(chunk_summed, c + 1)
                for k in range(BANKS):
                    act.wait_ge(banks_done, c * BANKS + (k + 2))
                    nodes = BANK * PAIR
                    nc.scalar.copy(counts[:, :, k * nodes:(k + 1) * nodes].rearrange("p q n -> p n q"),
                                   cps[k % RING][:, 0:nodes * NT].rearrange("p (n q) -> p n q", q=NT)
                                   ).then_inc(banks_free, 1)
                    if k in (9, 17, 24):
                        j = (9, 17, 24).index(k)
                        copy_sums(c * GPC + (LEAD * GPC + j), j)
                copy_keys(c + 1)

            with act.Fori(0, CHUNKS) as c:
                copy_chunk(c)
            copy_sums(FULL - 1, 0)
            copy_sums(FULL, 1)

            act.wait_ge(mode_ready, 1)
            with act.If(act.value_load(flag_i[0:1, 0:1], min_val=0, max_val=1) > 0):
                with act.Fori(0, PASSES * GROUPS) as n:
                    act.wait_ge(group_summed, n + 1)
                    nc.scalar.copy(sums[0:WINDOW, 0, :], eps[0]).then_inc(group_copied, 1)

            act.wait_ge(weights_loaded, 16 * (2 + HC))

            def relu(u, count):
                act.wait_ge(z_ready, count)
                for c in range(HC):
                    nc.scalar.activation(hidden[:, u, c, :], zps[u][:, c, 0:CHUNK], ACT.Relu,
                                         bias=b1c[:, c:c + 1]).then_inc(hidden_ready, 1)

            with act.Fori(0, CHUNKS // 2) as it:
                for u in range(2):
                    relu(u, it * 2 + (u + 1))
            relu(0, CHUNKS)
            for k, a in enumerate((st[:, 4:5], st[:, 9:10])):
                act.wait_ge(root_in, k + 1)
                nc.scalar.activation(a, a, ACT.Sqrt).then_inc(root_out, 1)

            act.wait_ge(affine_ready, 1)

            def activate(k, u, free, width):
                if free is not None:
                    act.wait_ge(out_turned, free)
                nc.scalar.activation(gelu[:, u, 0:width], h[:, bass.ds(k * (BLOCK * P), width)],
                                     ACT.Gelu_apprx_tanh, scale=st[:, 10:11], bias=st[:, 12:13]
                                     ).then_inc(act_ready, 1)

            activate(0, 0, None, BLOCK * P)
            activate(1, 1, None, BLOCK * P)
            with act.Fori(1, BLOCKS // 2) as it:
                for u in range(2):
                    activate(it * 2 + u, u, it * 2 + (u - 1), BLOCK * P)
            activate(BLOCKS, 0, BLOCKS - 1, LAST)
            act.wait_ge(root_in, 3)
            nc.scalar.activation(rstd[:, :], rstd[:, :], ACT.Sqrt).then_inc(root_out, 1)

        @block.tensor
        def _(pe):
            pe.wait_ge(consts_ready, 2)
            pe.wait_ge(diag_ready, 1)
            for k in range(2):
                last = nc.tensor.matmul(sps[:, k * P:(k + 1) * P], ones[:, :], diag[:, k, :],
                                        start=(k == 0), stop=(k == 1), skip_group_check=True)
            last.then_inc(base_summed, 1)
            pe.wait_ge(rows_ready, 1)
            rows = rows_f.rearrange("g (p j) -> g p j", j=TILES)
            for j in range(TILES):
                last = nc.tensor.transpose(banks[j // 4][:, (j % 4) * P:(j % 4 + 1) * P], rows[:, :, j], ident[:, :])
                if j % 4 == 3:
                    last.then_inc(turned, 1)

            def sum_tiles(u, s, k, first, tiles):
                oh = onehot[:, u % 2, :].rearrange("p (j w) -> p j w", w=WINDOW)
                for j in tiles:
                    last = nc.tensor.matmul(eps[s], oh[:, j, :], edges[:, u, j * D:(j + 1) * D],
                                            start=(k == 0 and j == 0), stop=(k == 1 and j == HALF - 1),
                                            skip_group_check=True)
                if tiles[-1] == HALF - 1:
                    last.then_inc(halves_free, 1)

            def begin_half(g, k, loaded, count):
                pe.wait_ge(onehot_ready, g * 2 + (k + 1))
                if k == 0:
                    pe.wait_ge(edges_added, g + 1)
                pe.wait_ge(loaded, count)

            def turn_sums(g, s):
                pe.wait_ge(sums_copied, g + 4)
                nc.tensor.transpose(turned_sum[s], sums[0:WINDOW, s, :], ident[0:WINDOW, 0:WINDOW]
                                    ).then_inc(sums_turned, 1)

            def three_groups(r, first=False):
                for j in range(GPC):
                    for k in range(2):
                        u = 2 * j + k
                        begin_half(r * GPC + j, k, edge_loaded[u], r * 16 + 16)
                        sum_tiles(u, j, k, None, range(HALF))
                    if not (first and j == 0):
                        turn_sums(r * GPC + (j - 1), (j - 1) % 3)

            for r in range(LEAD0):
                three_groups(r, r == 0)
            for s in range(SETS):
                pe.wait_ge(below_ready, s + 1)
                for c in range(CHUNKS):
                    last = nc.tensor.matmul(banks[2][0:PAIRS, c:c + 1], below[:, s % 2, c * PAIRS:(c + 1) * PAIRS],
                                            ones_b[:, :], start=(s == 0 and c == 0), stop=(s == SETS - 1),
                                            skip_group_check=True)
                last.then_inc(below_used, 1)
            with pe.Fori(LEAD0, LEAD) as r:
                three_groups(r)

            def turn_keys(c):
                pe.wait_ge(keys_made, c + 1)
                for at, rows in ((LO0, lo_f), (KEY0, node_f)):
                    last = nc.tensor.transpose(turn_ps[:, at:at + PAIRS], rows[0:PAIRS, :], ident[0:PAIRS, 0:PAIRS])
                last.then_inc(keys_turned, 1)

            turn_keys(0)

            def count_chunk(c):
                tiles = HPC * HALF // (BANKS - 1)
                for k in range(BANKS):
                    b = k // BPB
                    if k % BPB == 0:
                        pe.wait_ge(marks_ready, c * BATCHES + (b + 1))
                    if k >= RING:
                        pe.wait_ge(banks_free, c * BANKS + (k + 1 - RING))
                    for i in range(BANK):
                        n = (k % BPB) * BANK + i
                        last = nc.tensor.matmul(cps[k % RING][:, i * KEYS:(i + 1) * KEYS], mark_lo[b % 2][:, :, n],
                                                mark_key[b % 2][:, :, n], start=(i == 0), stop=(i == BANK - 1),
                                                skip_group_check=True)
                    last.then_inc(banks_done, 1)
                    if k < BANKS - 1:
                        t = k * tiles
                        u = t // HALF
                        g = c * GPC + (LEAD * GPC + u // 2)
                        if t % HALF == 0:
                            begin_half(g, u % 2, edge_loaded[u], (c + LEAD) * 16 + 16)
                        sum_tiles(u, u // 2, u % 2, None, range(t % HALF, t % HALF + tiles))
                        if (t + tiles) % (2 * HALF) == 0:
                            turn_sums(g - 1, (u // 2 - 1) % 3)
                    if k == 21:
                        pe.wait_ge(keys_ready, c * 2 + 2)
                        turn_keys(c + 1)
                pe.wait_ge(banks_free, (c + 1) * BANKS)
                pe.wait_ge(chunk_added, c + 1)
                for q in range(NT):
                    for part in (x_hi, x_lo):
                        last = nc.tensor.matmul(sps[:, 0:CHUNK], part[:, q, :], counts[:, q, :],
                                                start=(q == 0 and part is x_hi), stop=(q == NT - 1 and part is x_lo))
                last.then_inc(chunk_summed, 1)

            pe.wait_ge(x_split, 2)
            with pe.Fori(0, CHUNKS) as c:
                count_chunk(c)
            for g, loaded, count in ((FULL - 1, edge_loaded, (LEAD + CHUNKS) * 16 + 16), (FULL, None, 64)):
                for k in range(2):
                    u = 2 * (g - FULL + 1) + k
                    begin_half(g, k, loaded[u] if loaded else tail_loaded, count)
                    sum_tiles(u, g - FULL + 1, k, None, range(HALF))
                turn_sums(g - 1, (g - 1) % 3)
            turn_sums(FULL, 1)

            pe.wait_ge(cover_in, 1)
            nc.tensor.matmul(sps[:, 0:1], ones[:, :], st[:, 20:21], start=True, stop=True).then_inc(cover_summed, 1)

            pe.wait_ge(mode_ready, 1)
            with pe.If(pe.value_load(flag_i[0:1, 0:1], min_val=0, max_val=1) > 0):
                with pe.Fori(0, PASSES * GROUPS) as n:
                    pe.wait_ge(group_marked, n + 1)
                    pe.wait_ge(group_gathered, (n + 1) * (16 * TILES))
                    for i in range(4):
                        oh = onehot[:, i % 2, :].rearrange("p (j w) -> p j w", w=WINDOW)
                        for j in range(HALF):
                            last = nc.tensor.matmul(eps[0], oh[:, j, :], edges[:, i, j * D:(j + 1) * D],
                                                    start=(i == 0 and j == 0), stop=(i == 3 and j == HALF - 1))
                    last.then_inc(group_summed, 1)
                    pe.wait_ge(group_copied, n + 1)
                    nc.tensor.transpose(turned_sum[0], sums[0:WINDOW, 0, :], ident[0:WINDOW, 0:WINDOW]
                                        ).then_inc(group_turned, 1)
            pe.wait_ge(agg_ready, 1)
            pe.wait_ge(weights_loaded, 16 * (2 + HC))

            def up(c, u, free):
                if free is not None:
                    pe.wait_ge(hidden_ready, free)
                for k in range(HC):
                    last = nc.tensor.matmul(zps[u][:, k, 0:CHUNK], w1[:, k * P:(k + 1) * P],
                                            agg[:, bass.ds(c * CHUNK, CHUNK)], start=True, stop=True,
                                            skip_group_check=True)
                last.then_inc(z_ready, 1)

            def down(u, count, free):
                pe.wait_ge(hidden_ready, count)
                if free is not None:
                    pe.wait_ge(h_ready, free)
                for k in range(HC):
                    last = nc.tensor.matmul(hps[u][:, 0:CHUNK], w2[:, k, :], hidden[:, u, k, :],
                                            start=(k == 0), stop=(k == HC - 1))
                last.then_inc(h_summed, 1)

            up(0, 0, None)
            up(1, 1, None)
            down(0, HC, None)
            up(2, 0, HC)
            down(1, 2 * HC, None)
            with pe.Fori(0, (CHUNKS - 3) // 2) as it:
                for u in range(2):
                    up(it * 2 + (u + 3), 1 - u, it * (2 * HC) + (u + 2) * HC)
                    down(u, it * (2 * HC) + (u + 3) * HC, it * 2 + (u + 1))
            down(0, CHUNKS * HC, CHUNKS - 2)

            for k in range(2):
                pe.wait_ge(mean_in, k + 1)
                nc.tensor.matmul(turn_ps[:, k:k + 1], ones[:, :], st[:, k:k + 1],
                                 start=True, stop=True, skip_group_check=True).then_inc(mean_summed, 1)

            def turn(u, count, free):
                pe.wait_ge(act_ready, count)
                if free is not None:
                    pe.wait_ge(y_ready, free)
                for t in range(BLOCK):
                    last = nc.tensor.transpose(ops[u][:, t * P:(t + 1) * P], gelu[:, u, t * P:(t + 1) * P],
                                               ident[:, :])
                last.then_inc(out_turned, 1)

            turn(0, 1, None)
            turn(1, 2, None)
            with pe.Fori(1, BLOCKS // 2) as it:
                for u in range(2):
                    turn(u, it * 2 + (u + 1), it * 2 + (u - 1))
            pe.wait_ge(act_ready, BLOCKS + 1)
            pe.wait_ge(y_ready, BLOCKS - 1)
            nc.tensor.transpose(ops[0][0:LAST, 0:P], gelu[:, 0, 0:LAST], ident[:, :]).then_inc(out_turned, 1)

        @block.vector
        def _(dve):
            steps = [0]

            def link(ins, chain, count):
                count[0] += 1
                ins.then_inc(chain, 1)
                dve.wait_ge(chain, count[0])

            dve.memset(rows_i[96:P, :], -1).then_inc(rows_padded, 1)
            dve.memset(late[:, :, :], -1)
            link(dve.memset(tile_end_i[:, :], 2 * N), setup, steps)
            link(dve.memset(late[:, 0, :], 0), setup, steps)
            dve.engine_nop().then_inc(rows_padded, 1)
            link(dve.memset(x_raw[96:P, (NT - 1) * D:NT * D], 0.0), setup, steps)
            dve.engine_nop().then_inc(rows_padded, 1)
            dve.memset(lo[:, :], 0.0)
            link(dve.memset(hi[:, :], 0.0), setup, steps)
            dve.wait_ge(consts_ready, 1)
            dve.tensor_copy(iota_f[:, :], iota_i[:, :])
            dve.tensor_copy(pair_f[:, :], pair_i[:, :])
            link(dve.tensor_copy(prow_f[:, :], prow_i[:, :]), setup, steps)
            dve.tensor_scalar(ident[:, :], iota_f[:, :], prow_f[:, 0:1], None, ALU.is_equal
                              ).then_inc(consts_ready, 1)

            link(dve.memset(rows_f[96:P, :], 0.0), setup, steps)
            dve.wait_ge(dst_loaded, 32)
            link(dve.tensor_copy(rows_f[0:GROUPS, :], rows_i[0:GROUPS, :]), setup, steps)
            dve.tensor_reduce(hi[0:GROUPS, :], rows_f[0:GROUPS, :], AX_X, ALU.max)
            link(dve.tensor_scalar(pad_f[0:GROUPS, :], rows_f[0:GROUPS, REST:GROUP], 0.0, PAD,
                                   ALU.is_lt, ALU.mult), setup, steps)
            link(dve.tensor_tensor(rows_f[0:GROUPS, REST:GROUP], rows_f[0:GROUPS, REST:GROUP],
                                   pad_f[0:GROUPS, :], ALU.add), setup, steps)
            dve.engine_nop().then_inc(rows_ready, 1)
            link(dve.tensor_reduce(lo[0:GROUPS, :], rows_f[0:GROUPS, :], AX_X, ALU.min), setup, steps)
            link(dve.tensor_tensor(hi[:, :], hi[:, :], lo[:, :], ALU.subtract), setup, steps)
            dve.tensor_scalar(diag[:, 0, :], ident[:, :], lo[:, 0:1], None, ALU.mult)
            dve.tensor_scalar(diag[:, 1, :], ident[:, :], hi[:, 0:1], None, ALU.mult).then_inc(diag_ready, 1)

            dve.wait_ge(base_summed, 1)
            dve.tensor_copy(base_i[:, :], sps[0:1, 0:P])
            dve.tensor_copy(base_f[:, :], sps[:, 0:P])
            link(dve.tensor_reduce(wide[:, 0:1], sps[:, P:2 * P], AX_X, ALU.max), setup, steps)

            for q in range(TILES // 4):
                dve.wait_ge(turned, q + 1)
                dve.tensor_tensor(dst_cols[:, q * 4:q * 4 + 4, :],
                                  banks[q][:, :].rearrange("p (j g) -> p j g", g=P)[:, :, 0:GROUPS],
                                  base_f[:, 0:GROUPS].rearrange("p (a g) -> p a g", a=1).to_broadcast([P, 4, GROUPS]),
                                  ALU.subtract).then_inc(setup, 1)
            steps[0] += TILES // 4
            dve.wait_ge(setup, steps[0])
            link(dve.memset(agg[:, :], 0.0), setup, steps)

            window = iota_f[:, 0:WINDOW].rearrange("p (a w) -> p a w", a=1).to_broadcast([P, HALF, WINDOW])

            def mark(g, k):
                dve.wait_ge(halves_free, g * 2 + (k + HALVES - 1))
                oh = onehot[:, k, :].rearrange("p (j w) -> p j w", w=WINDOW)
                dve.tensor_tensor(oh, window, dst_cols[:, k * HALF:(k + 1) * HALF, bass.ds(g, 1)
                                                       ].to_broadcast([P, HALF, WINDOW]),
                                  ALU.is_equal).then_inc(onehot_ready, 1)

            def add(g, s, chunks=None):
                base = dve.value_load(base_i[0:1, bass.ds(g, 1)], min_val=0, max_val=N - 1)
                dve.wait_ge(sums_turned, g + 4)
                dve.wait_ge(edges_added, g + 3)
                if chunks is not None:
                    dve.wait_ge(chunk_added, chunks)
                at = agg[:, bass.ds(base, WINDOW)]
                dve.tensor_tensor(at, at, turned_sum[s], ALU.add).then_inc(edges_added, 1)

            def three_groups(r, first=False):
                for j in range(GPC):
                    mark(r * GPC + j, 0)
                    if not first:
                        add(r * GPC + (j - GPC), j)
                    mark(r * GPC + j, 1)

            three_groups(0, True)
            three_groups(1)

            dve.wait_ge(x_high, 1)
            xr = x_raw.rearrange("p (t d) -> p t d", d=D)
            link(dve.tensor_tensor(x_lo[:, :, :], xr, x_hi[:, :, :].bitcast(F32), ALU.subtract), setup, steps)
            dve.engine_nop().then_inc(x_split, 2)

            dve.wait_ge(ends_loaded, 32)
            link(dve.tensor_scalar(tile_end[:, :], tile_end_i[:, :], 1.0 / PAIR, None, ALU.mult), setup, steps)
            dve.wait_ge(consts_ready, 3)
            for s in range(SETS):
                if s >= 2:
                    dve.wait_ge(below_used, s - 1)
                dve.tensor_scalar(below[:, s % 2, :], pair_row, tile_end[:, s:s + 1], None, ALU.is_gt
                                  ).then_inc(below_ready, 1)
            dve.memset(tile_f[:, :], 0.0).then_inc(setup, 1)
            steps[0] += 1
            dve.wait_ge(setup, steps[0])
            dve.wait_ge(below_used, SETS)
            link(dve.tensor_scalar(tile_f[0:PAIRS, 0:CHUNKS], banks[2][0:PAIRS, 0:CHUNKS], float(ET - 1), None, ALU.min),
                 setup, steps)
            for v in range(P):
                dve.memset(values[:, v, :], float(v))
            dve.memset(turned_lo[:, :, :], -1.0)
            link(dve.memset(turned_key[:, :, :], -1.0), setup, steps)
            dve.engine_nop().then_inc(pads_ready, 1)

            def prep_chain(ins, count):
                ins.then_inc(prep, 1)
                dve.wait_ge(prep, count)

            STEPS = 8

            def stage_tile(c):
                dve.tensor_copy(tile_slot[0:PAIRS, :], tile_f[0:PAIRS, bass.ds(c, 1)]).then_inc(tile_staged, 1)

            def stage_row(c):
                dve.wait_ge(begins_loaded, c * 16 + 16)
                n = c * STEPS
                prep_chain(dve.tensor_scalar(junk[0:PAIRS, :], begins[0:PAIRS, :], pair_f[0:PAIRS, bass.ds(c, 1)], 0.0,
                                             ALU.is_lt, ALU.add, accum_out=first_f[0:PAIRS, :]), n + 1)
                prep_chain(dve.scalar_tensor_tensor(first_i[0:PAIRS, :], tile_f[0:PAIRS, bass.ds(c, 1)], float(P),
                                                    first_f[0:PAIRS, :], ALU.mult, ALU.add), n + 2)
                dve.tensor_scalar(row_slot[0:PAIRS, :], first_i[0:PAIRS, :], 4, None, ALU.arith_shift_right
                                  ).then_inc(row_staged, 1)

            def make_keys(c):
                dve.wait_ge(near_loaded, c * 32 + 32)
                n = c * STEPS + 2
                s, d = near[0:PAIRS, 0, :], near[0:PAIRS, 1, :]
                dve.tensor_scalar(node_f[0:PAIRS, :], d, pair_f[0:PAIRS, bass.ds(c, 1)], None, ALU.subtract
                                  ).then_inc(prep, 1)
                dve.tensor_scalar(lo_i[0:PAIRS, :], s, P - 1, None, ALU.bitwise_and).then_inc(prep, 1)
                prep_chain(dve.tensor_scalar(hi_i[0:PAIRS, :], s, SHIFT, None, ALU.arith_shift_right), n + 3)
                dve.scalar_tensor_tensor(junk[0:PAIRS, :], node_f[0:PAIRS, :], -1.0, node_f[0:PAIRS, :],
                                         ALU.add, ALU.mult).then_inc(prep, 1)
                dve.tensor_copy(lo_f[0:PAIRS, :], lo_i[0:PAIRS, :]).then_inc(prep, 1)
                prep_chain(dve.scalar_tensor_tensor(node_f[0:PAIRS, :], node_f[0:PAIRS, :], float(NT), hi_i[0:PAIRS, :],
                                                    ALU.mult, ALU.add), n + 6)
                dve.tensor_scalar(junk[0:PAIRS, :], junk[0:PAIRS, :], 0.0, 0.0, ALU.is_equal, ALU.add,
                                  accum_out=covered[0:PAIRS, bass.ds(c, 1)]).then_inc(keys_made, 1)
                dve.wait_ge(keys_made, c + 1)

            def mark_batch(c, b):
                if b == 0:
                    dve.wait_ge(keys_ready, c * 2 + 2)
                    dve.wait_ge(banks_done, c * BANKS + 1)
                if b >= 2:
                    dve.wait_ge(banks_done, c * BANKS + (BPB * (b - 1) + 1))
                for rows, to, n in ((turned_lo, mark_lo, P), (turned_key, mark_key, KEYS)):
                    last = dve.tensor_tensor(to[b % 2], values[:, 0:n, :],
                                             rows[:, b:b + 1, :].to_broadcast([P, n, BP]), ALU.is_equal)
                last.then_inc(marks_ready, 1)

            with dve.Fori(2, 4) as r:
                three_groups(r)
            stage_tile(0)
            three_groups(4)
            stage_row(0)
            with dve.Fori(5, LEAD) as r:
                three_groups(r)
            make_keys(0)

            def head(c):
                stage_tile(c + 1)
                mark(c * GPC + LEAD * GPC, 0)
                mark_batch(c, 0)

            def rest(c):
                g = c * GPC + LEAD * GPC
                add(g - GPC, 0, c + 1)
                mark(g, 1)
                mark_batch(c, 1)
                stage_row(c + 1)
                mark(g + 1, 0)
                add(g + (1 - GPC), 1)
                mark_batch(c, 2)
                mark(g + 1, 1)
                mark_batch(c, 3)
                make_keys(c + 1)
                mark(g + 2, 0)
                add(g + (2 - GPC), 2)
                mark_batch(c, 4)
                mark(g + 2, 1)

            def add_chunk(c):
                dve.wait_ge(chunk_summed, c + 2)
                dve.wait_ge(edges_added, c * GPC + (LEAD * GPC + 3))
                at = agg[:, bass.ds(c * CHUNK, CHUNK)]
                dve.tensor_tensor(at, at, sps[:, 0:CHUNK], ALU.add).then_inc(chunk_added, 1)

            head(0)
            with dve.Fori(0, CHUNKS - 1) as c:
                rest(c)
                head(c + 1)
                add_chunk(c)
            rest(CHUNKS - 1)
            for g in (FULL - 1, FULL):
                mark(g, 0)
                if g == FULL - 1:
                    add_chunk(CHUNKS - 1)
                add(g - 3, (g - 3) % 3, CHUNKS + 1)
                mark(g, 1)
            for g in range(FULL - 2, GROUPS):
                add(g, g % 3)
            dve.wait_ge(edges_added, GROUPS + 3)

            steps = [0]

            def step(ins):
                link(ins, norm, steps)

            step(dve.memset(st[:, 20:21], 0.0))
            step(dve.tensor_reduce(st[0:PAIRS, 20:21], covered[0:PAIRS, :], AX_X, ALU.add))
            dve.engine_nop().then_inc(cover_in, 1)
            dve.wait_ge(cover_summed, 1)
            step(dve.tensor_scalar(wide[:, 1:2], sps[:, 0:1], float(E), None, ALU.not_equal))
            step(dve.tensor_scalar(wide[:, 0:1], wide[:, 0:1], float(WINDOW), None, ALU.is_ge))
            step(dve.tensor_tensor(wide[:, 0:1], wide[:, 0:1], wide[:, 1:2], ALU.max))
            step(dve.tensor_copy(flag_i[:, :], wide[0:1, 0:1]))
            dve.engine_nop().then_inc(mode_ready, 1)

            with dve.If(dve.value_load(flag_i[0:1, 0:1], min_val=0, max_val=1) > 0):
                dve.memset(agg[:, :], 0.0).then_inc(agg_clear, 1)
                dve.memset(pass_base[:, :], -float(WINDOW)).then_inc(agg_clear, 1)
                dve.wait_ge(agg_clear, 2)
                with dve.Fori(0, PASSES) as w:
                    dve.tensor_scalar(pass_base[:, :], pass_base[:, :], float(WINDOW), None, ALU.add
                                      ).then_inc(agg_clear, 1)
                    dve.wait_ge(agg_clear, w + 3)
                    dve.sem_inc(passes_begun, 1)
                    with dve.Fori(0, GROUPS) as g:
                        n = w * GROUPS + g
                        dve.memset(edge_dst[:, :], -1)
                        dve.memset(edge_src[:, :], 0).then_inc(slots_clear, 1)
                        dve.wait_ge(group_loaded, (n + 1) * 128)
                        dve.tensor_scalar(edge_dst_f[:, :], edge_dst[:, :], pass_base[:, 0:1], None, ALU.subtract
                                          ).then_inc(gchain, 1)
                        dve.wait_ge(gchain, n + 1)
                        for k in range(2):
                            oh = onehot[:, k, :].rearrange("p (j w) -> p j w", w=WINDOW)
                            near_k = edge_dst_f[:, k * HALF:(k + 1) * HALF].rearrange("p (j a) -> p j a", a=1)
                            last = dve.tensor_tensor(oh, window, near_k.to_broadcast([P, HALF, WINDOW]), ALU.is_equal)
                        last.then_inc(group_marked, 1)
                        dve.wait_ge(group_turned, n + 1)
                        at = agg[:, bass.ds(w * WINDOW, WINDOW)]
                        dve.tensor_tensor(at, at, turned_sum[0], ALU.add).then_inc(group_added, 1)
                        dve.wait_ge(group_added, n + 1)
            dve.engine_nop().then_inc(agg_ready, 1)

            dve.wait_ge(params_loaded, 16 * 6)
            def keep(c, u, count):
                hc = h[:, bass.ds(c * CHUNK, CHUNK)]
                dve.wait_ge(h_summed, count)
                dve.tensor_scalar(hc, hps[u][:, 0:CHUNK], par[:, B2:B2 + 1], None, ALU.add).then_inc(h_ready, 1)
                dve.wait_ge(h_ready, count)
                dve.bn_stats(stats[:, bass.ds(c, 1), :].rearrange("p a s -> p (a s)"), hc).then_inc(h_stats, 1)

            with dve.Fori(0, CHUNKS // 2) as it:
                for u in range(2):
                    keep(it * 2 + u, u, it * 2 + (u + 1))
            keep(CHUNKS - 1, 0, CHUNKS)
            dve.wait_ge(h_stats, CHUNKS)

            def c(k):
                return st[:, k:k + 1]

            m, v = mv[:, 0:1], mv[:, 1:2]
            step(dve.bn_aggr(mv[:, :], stats[:, :, :].rearrange("p c s -> p (c s)")))
            dve.tensor_scalar(c(0), m, 1.0 / D, None, ALU.mult).then_inc(mean_in, 1)
            dve.wait_ge(mean_summed, 1)
            step(dve.tensor_tensor(c(2), m, turn_ps[:, 0:1], ALU.subtract))
            step(dve.tensor_tensor(c(3), c(2), c(2), ALU.mult))
            step(dve.tensor_tensor(c(3), c(3), v, ALU.add))
            dve.tensor_scalar(c(1), c(3), 1.0 / D, None, ALU.mult).then_inc(mean_in, 1)
            dve.wait_ge(mean_summed, 2)
            dve.tensor_scalar(c(4), turn_ps[:, 1:2], EPS, None, ALU.add).then_inc(root_in, 1)
            dve.wait_ge(root_out, 1)
            step(dve.reciprocal(c(4), c(4)))
            step(dve.tensor_tensor(c(5), c(4), par[:, LNW:LNW + 1], ALU.mult))
            step(dve.tensor_scalar(c(6), c(2), c(5), par[:, LNB:LNB + 1], ALU.mult, ALU.add))
            step(dve.tensor_tensor(c(7), c(6), par[:, GNM:GNM + 1], ALU.mult))
            step(dve.tensor_tensor(c(7), c(6), c(7), ALU.subtract))
            step(dve.tensor_tensor(c(8), c(7), c(7), ALU.mult))
            step(dve.tensor_tensor(c(9), c(5), c(5), ALU.mult))
            step(dve.scalar_tensor_tensor(c(9), v, c(9), c(8), ALU.mult, ALU.add))
            dve.tensor_scalar(c(9), c(9), EPS, None, ALU.add).then_inc(root_in, 1)
            dve.wait_ge(root_out, 2)
            step(dve.reciprocal(c(9), c(9)))
            step(dve.tensor_tensor(c(9), c(9), par[:, GNW:GNW + 1], ALU.mult))
            step(dve.tensor_tensor(c(10), c(5), c(9), ALU.mult))
            step(dve.tensor_scalar(c(11), c(7), c(9), par[:, GNB:GNB + 1], ALU.mult, ALU.add))
            step(dve.tensor_tensor(c(12), c(10), m, ALU.mult))
            step(dve.tensor_tensor(c(12), c(11), c(12), ALU.subtract))
            dve.engine_nop().then_inc(affine_ready, 1)

            dve.wait_ge(xs_loaded, 32)

            def finish(t0, u, count, tiles, rows):
                y = xs[0:rows, bass.ds(t0, tiles), :]
                dve.wait_ge(out_turned, count)
                got = ops[u][0:rows, 0:tiles * P].rearrange("p (t d) -> p t d", d=P)
                dve.scalar_tensor_tensor(y, y, 2.0, got, ALU.mult, ALU.add).then_inc(y_ready, 1)
                dve.wait_ge(y_ready, count)
                for t in range(tiles):
                    dve.bn_stats(lnstats[0:rows, bass.ds(t0 + t, 1), :].rearrange("p a s -> p (a s)"),
                                 xs[0:rows, bass.ds(t0 + t, 1), :].rearrange("p a d -> p (a d)")
                                 ).then_inc(ln_stats, 1)

            dve.memset(lnstats[:, NT - 1, :], 1.0).then_inc(ln, 1)
            dve.wait_ge(ln, 1)
            with dve.Fori(0, BLOCKS // 2) as it:
                for u in range(2):
                    finish(it * (2 * BLOCK) + u * BLOCK, u, it * 2 + (u + 1), BLOCK, P)
            finish(NT - 1, 0, BLOCKS + 1, 1, LAST)
            dve.wait_ge(ln_stats, NT)

            steps = [1]

            def lnstep(ins):
                link(ins, ln, steps)

            even, odd = lnstats[:, :, 1], lnstats[:, :, 4]
            dve.tensor_tensor(lngap[:, :], even, odd, ALU.subtract)
            lnstep(dve.tensor_tensor(lnmean[:, :], even, odd, ALU.add))
            dve.tensor_scalar(lnmean[:, :], lnmean[:, :], 0.5, None, ALU.mult)
            dve.tensor_tensor(rstd[:, :], lnstats[:, :, 2], lnstats[:, :, 5], ALU.add)
            lnstep(dve.tensor_tensor(lngap[:, :], lngap[:, :], lngap[:, :], ALU.mult))
            dve.tensor_scalar(lngap[:, :], lngap[:, :], 0.25, EPS, ALU.mult, ALU.add)
            lnstep(dve.tensor_scalar(rstd[:, :], rstd[:, :], 1.0 / D, None, ALU.mult))
            dve.tensor_tensor(rstd[:, :], rstd[:, :], lngap[:, :], ALU.add).then_inc(root_in, 1)
            dve.wait_ge(root_out, 3)
            lnstep(dve.reciprocal(rstd[:, :], rstd[:, :]))

            def normalise(t, rows):
                yt = xs[0:rows, bass.ds(t, 1), :].rearrange("p a d -> p (a d)")
                dve.tensor_scalar(yt, yt, lnmean[0:rows, bass.ds(t, 1)], rstd[0:rows, bass.ds(t, 1)],
                                  ALU.subtract, ALU.mult).then_inc(out_ready, 1)

            with dve.Fori(0, BLOCKS) as k:
                for t in range(BLOCK):
                    normalise(k * BLOCK + t, P)
            normalise(NT - 1, LAST)


_INS = ['x', 'src', 'dst', 'edge_attr_128', 'L0_gnn_W1', 'L0_gnn_b1', 'L0_gnn_W2', 'L0_gnn_b2', 'L0_gnn_ln_w',
        'L0_gnn_ln_b', 'L0_gnn_gn_w', 'L0_gnn_gn_b', 'L0_gnn_gn_ms']
_OUTS = [((6250, 128), 'float32')]


def kernel(**inputs):
    import numpy as _np
    import concourse.bacc as _bacc
    from concourse import mybir as _mybir
    from concourse.bass_utils import run_bass_kernel_spmd as _run

    nc = _bacc.Bacc("TRN2", target_bir_lowering=False, num_devices=1)
    arrays, args = {}, []
    for name in _INS:
        a = _np.ascontiguousarray(inputs[name])
        arrays[f"in_{name}_dram"] = a
        args.append(nc.dram_tensor(f"in_{name}_dram", a.shape, _mybir.dt.from_np(a.dtype), kind="ExternalInput").ap())
    for i, (shape, dtype) in enumerate(_OUTS):
        dt = _mybir.dt.from_np(_np.dtype(dtype))
        args.append(nc.dram_tensor(f"out_{i}_dram", shape, dt, kind="ExternalOutput").ap())
    gnn_kernel(nc, *args)
    r = _run(nc, [arrays], core_ids=[0])
    got = tuple(r.results[0][f"out_{i}_dram"] for i in range(len(_OUTS)))
    return got[0]
```

```python
from contextlib import ExitStack

import concourse.bass as bass
from concourse import mybir

ALU = mybir.AluOpType
ACT = mybir.ActivationFunctionType
F32 = mybir.dt.float32
F32R = mybir.dt.float32r
BF16 = mybir.dt.bfloat16
I32 = mybir.dt.int32
I16 = mybir.dt.int16
AX_X = mybir.AxisListType.X

P = 128
EPS = 1e-5

TILES = 16
GROUP = P * TILES
WINDOW = 72
HALF = TILES // 2
HALVES = 6
PLACES = 3
GPC = 3
HPC = 2 * GPC
PAD = 1.0e6

PAIR = 2
STRIDE = 16
CHUNK = 250
PAIRS = CHUNK // PAIR
BATCH = 25
BATCHES = PAIRS // BATCH
BP = BATCH + 1
MARKED = 3
BANK = 5
BANKS = PAIRS // BANK
BPB = BATCH // BANK
CREDIT = BPB + 1
RING = 3
SHIFT = 7
DST_SHIFT = 13
NO_EDGE = (1 << 30) - 1

KEYS_AT = 20
BELOW = 3
SEARCH = 13
PIECE = 7

OPS = 4
ACT_TILES = 2
BLOCK = 4


def gnn_kernel(nc, x, src, dst, edge_attr, W1, b1, W2, b2, ln_w, ln_b, gn_w, gn_b, gn_ms, out):
    N, D = x.shape
    E = src.shape[0]
    H = W1.shape[1]
    HC = H // P
    FULL = E // GROUP
    REST = E - FULL * GROUP
    REST_P, REST_E = REST // TILES, REST % TILES
    GROUPS = FULL + 1
    CHUNKS = N // CHUNK
    LEAD = (FULL // GPC) - CHUNKS
    LEAD0 = 2
    assert D == P and REST and REST_E > HALF and GROUPS <= P and FULL == (LEAD + CHUNKS) * GPC + 1
    assert CHUNKS * CHUNK == N and CHUNKS % 2 == 1 and LEAD > LEAD0 + 3
    PASSES = -(-N // WINDOW)
    NT = -(-N // P)
    LAST = N - (NT - 1) * P
    BLOCKS = (NT - 1) // BLOCK
    assert PIECE * (LEAD - 1) == NT
    assert BLOCKS * BLOCK == NT - 1 and BLOCKS % 2 == 0
    KEYS = PAIR * NT
    SPAN = 2 * P
    ET = E // SPAN
    SETS = -(-ET // P)
    NPAIR = N // PAIR
    ROWS = E // STRIDE + 1
    AT_ONCE = 3
    PARTS = LEAD0 * GPC + AT_ONCE
    LISTED = (ROWS - 1) * STRIDE + P
    assert N <= 1 << DST_SHIFT and 0 < LISTED - E <= P and (ET * SPAN + P) // STRIDE < ROWS and STRIDE == 1 << 4

    listed = nc.dram_tensor("listed", (LISTED,), I32, kind="Internal").ap()
    listed_rows = nc.dram_tensor("listed_rows", (ROWS, P), I32, kind="Internal").ap()

    with ExitStack() as ctx:
        def sb(name, shape, dt=F32):
            return ctx.enter_context(nc.sbuf_tensor(name, shape, dt))

        def psum(name, shape, dt=F32):
            return ctx.enter_context(nc.psum_tensor(name, shape, dt))

        def sem(name):
            return ctx.enter_context(nc.semaphore(name))

        edges = sb("edges", [P, HALVES, HALF * D])
        onehot = sb("onehot", [P, PLACES, HALF * WINDOW])
        counts = sb("counts", [P, NT, CHUNK], F32R)
        x_hi = sb("x_hi", [P, NT, D], F32R)
        x_lo = sb("x_lo", [P, NT, D], F32R)
        LW = P * BP
        KW = KEYS * BP
        pool_m = sb("pool_m", [P, max(2 * NT * D, MARKED * (LW + KW))], BF16)
        mark_lo = [pool_m[:, s * (LW + KW):s * (LW + KW) + LW].rearrange("p (v n) -> p v n", n=BP)
                   for s in range(MARKED)]
        mark_key = [pool_m[:, s * (LW + KW) + LW:(s + 1) * (LW + KW)].rearrange("p (v n) -> p v n", n=BP)
                    for s in range(MARKED)]
        x_raw = pool_m[:, 0:2 * NT * D].bitcast(F32)
        xs = x_raw.rearrange("p (t d) -> p t d", d=D)
        behind = pool_m[:, 2 * NT * D:MARKED * (LW + KW)]
        below = behind[:, 0:BELOW * SEARCH * PAIRS].rearrange("p (s v) -> p s v", s=BELOW)
        behind_f = behind.bitcast(F32)
        lnstats = behind_f[:, 0:6 * NT].rearrange("p (t s) -> p t s", s=6)
        lnmean, lngap, rstd = [behind_f[:, k * NT:(k + 1) * NT] for k in (6, 7, 8)]
        lnmean_act = behind_f[:, 9 * NT:10 * NT]
        stats = behind_f[:, 10 * NT:10 * NT + 6 * CHUNKS].rearrange("p (c s) -> p c s", s=6)
        values = sb("values", [P, P, BP], BF16)
        pair_row = values[:, :, :].rearrange("p v n -> p (v n)")[:, 0:NPAIR + 7].bitcast(I16)
        agg = sb("agg", [P, N + WINDOW])
        h = agg[:, 0:N]
        rows_f = agg[:, 0:GROUP]
        rows_i = agg[:, GROUP:2 * GROUP].bitcast(I32)
        src_rows = agg[:, 2 * GROUP:3 * GROUP].bitcast(I32)
        pad_f = onehot[:, :, :].rearrange("p s e -> p (s e)")[:, 0:GROUP - REST]
        dst_cols = sb("dst_cols", [P, TILES, GROUPS], BF16)
        hidden = onehot[:, :, :].rearrange("p s e -> p (s e)")[:, 0:2 * HC * CHUNK].rearrange(
            "p (u k n) -> p u k n", u=2, k=HC)
        gelu = behind_f[:, 10 * NT + 6 * CHUNKS:10 * NT + 6 * CHUNKS + 2 * BLOCK * P].rearrange("p (u n) -> p u n", u=2)
        w1 = sb("w1", [P, H])
        w2 = sb("w2", [P, HC, D])
        b1c = sb("b1c", [P, HC])
        par = sb("par", [P, 6])
        B2, LNW, LNB, GNW, GNB, GNM = range(6)
        iota_f = sb("iota_f", [P, P])
        prow_i = sb("prow_i", [P, 1], I32)
        prow_f = sb("prow_f", [P, 1])
        pair_i = sb("pair_i", [P, CHUNKS + 1], I32)
        pair_f = sb("pair_f", [P, CHUNKS + 1])
        pair_w = sb("pair_w", [P, CHUNKS + 1])
        tile_end_i = sb("tile_end_i", [P, SETS], I32)
        tile_end = sb("tile_end", [P, SETS])
        tile_f = sb("tile_f", [P, CHUNKS + 1])
        tile_rows = sb("tile_rows", [P, CHUNKS + 1, 2], I32)
        tile_slot = sb("tile_slot", [P, 2], I32)
        row_slot = sb("row_slot", [P, 1], I32)
        first_i = sb("first_i", [P, 1], I32)
        first_f = sb("first_f", [P, 1])
        begins = sb("begins", [P, SPAN], I32)
        near = begins[:, 0:P]
        iota_i = begins[:, 0:P]
        junk = sb("junk", [P, SPAN])
        lo_i = sb("lo_i", [P, P], I32)
        hi_i = sb("hi_i", [P, P], I32)
        node_i = junk[:, P:2 * P].bitcast(I32)
        no_edges = lo_i[0:1, :]
        lo_f = sb("lo_f", [P, P])
        node_f = sb("node_f", [P, P])
        covered = sb("covered", [P, CHUNKS + 1])
        turned_lo = sb("turned_lo", [P, BATCHES, BP], BF16)
        turned_key = sb("turned_key", [P, BATCHES, BP], BF16)
        ident = sb("ident", [P, P])
        ones = sb("ones", [P, P])
        ones_b = sb("ones_b", [P, 1], BF16)
        lo = sb("lo", [P, 1])
        hi = sb("hi", [P, 1])
        base_f = lo_f
        base_i = sb("base_i", [1, P], I32)
        wide = sb("wide", [P, 2])
        flag_i = sb("flag_i", [1, 1], I32)
        sums = sb("sums", [WINDOW, D])
        diag = junk[:, :].rearrange("p (k n) -> p k n", k=2)
        edge_dst, edge_src = lo_i[:, 0:TILES], hi_i[:, 0:TILES]
        edge_dst_f = junk[:, 0:TILES]
        pass_base = sb("pass_base", [P, 1])
        mv = sb("mv", [P, 2])
        st = sb("st", [P, 24])

        banks = [psum(f"bank{i}", [P, 512]) for i in range(8)]
        cps = banks[0:RING]
        eps = [b[0:WINDOW, 0:D] for b in banks[3:6]]
        turned_sum = [b[:, D:D + WINDOW] for b in banks[3:6]]
        turn_ps, sps = banks[6], banks[7]
        KEY0, LO0 = 0, P
        zps = [banks[u][:, :].rearrange("p (k n) -> p k n", k=HC) for u in range(2)]
        hps = [banks[2], banks[3]]
        ops = [banks[4], sps, banks[0], banks[1]]

        DST_AT = 5
        ROWS_READ = 10

        rows_padded = sem("rows_padded")
        dst_loaded = sem("dst_loaded")
        ends_loaded = sem("ends_loaded")
        src_loaded = sem("src_loaded")
        listed_ready = sem("listed_ready")
        listed_stored = sem("listed_stored")
        table_built = sem("table_built")
        x_loaded = sem("x_loaded")
        x_high = sem("x_high")
        x_split = sem("x_split")
        consts_ready = sem("consts_ready")
        setup = sem("setup")
        diag_ready = sem("diag_ready")
        base_summed = sem("base_summed")
        rows_ready = sem("rows_ready")
        turned = sem("turned")
        agg_zeroed = sem("agg_zeroed")
        pair_row_ready = sem("pair_row_ready")
        below_ready = sem("below_ready")
        below_used = sem("below_used")
        edge_loaded = [sem(f"edge_loaded{i}") for i in range(HALVES)]
        tail_loaded = sem("tail_loaded")
        onehot_ready = sem("onehot_ready")
        halves_free = sem("halves_free")
        sums_copied = sem("sums_copied")
        sums_turned = sem("sums_turned")
        edges_added = sem("edges_added")
        tile_staged = sem("tile_staged")
        row_staged = sem("row_staged")
        gathers_begun = sem("gathers_begun")
        begins_loaded = sem("begins_loaded")
        near_loaded = sem("near_loaded")
        prep = sem("prep")
        keys_made = sem("keys_made")
        keys_turned = sem("keys_turned")
        keys_ready = sem("keys_ready")
        pads_ready = sem("pads_ready")
        marks_ready = sem("marks_ready")
        banks_done = sem("banks_done")
        banks_free = sem("banks_free")
        chunk_summed = sem("chunk_summed")
        chunk_added = sem("chunk_added")
        cover_in = sem("cover_in")
        cover_summed = sem("cover_summed")
        mode_ready = sem("mode_ready")
        agg_clear = sem("agg_clear")
        slots_clear = sem("slots_clear")
        group_loaded = sem("group_loaded")
        group_gathered = sem("group_gathered")
        group_marked = sem("group_marked")
        group_summed = sem("group_summed")
        group_copied = sem("group_copied")
        group_turned = sem("group_turned")
        group_added = sem("group_added")
        gchain = sem("gchain")
        passes_begun = sem("passes_begun")
        agg_ready = sem("agg_ready")
        weights_loaded = sem("weights_loaded")
        params_loaded = sem("params_loaded")
        xs_loaded = sem("xs_loaded")
        z_ready = sem("z_ready")
        hidden_ready = sem("hidden_ready")
        h_summed = sem("h_summed")
        h_ready = sem("h_ready")
        h_stats = sem("h_stats")
        norm = sem("norm")
        mean_in = sem("mean_in")
        mean_summed = sem("mean_summed")
        affine_ready = sem("affine_ready")
        act_ready = sem("act_ready")
        out_turned = sem("out_turned")
        y_ready = sem("y_ready")
        ln_stats = sem("ln_stats")
        ln = sem("ln")
        root_in = sem("root_in")
        root_out = sem("root_out")
        scales_ready = sem("scales_ready")
        out_ready = sem("out_ready")
        act_out_ready = sem("act_out_ready")
        out_stored = sem("out_stored")

        HD = HALF * D
        edge_full = edge_attr[0:FULL * GROUP, :].rearrange("(g p j) d -> g p (j d)", p=P, j=TILES)
        rest0 = FULL * GROUP
        edge_rest = edge_attr[rest0:rest0 + REST_P * TILES, :].rearrange("(p j) d -> p (j d)", j=TILES)
        edge_last = edge_attr[rest0 + REST_P * TILES:E, :].rearrange("(a j) d -> a (j d)", a=1)
        dst_full = dst[0:FULL * GROUP].rearrange("(g e) -> g e", e=GROUP)
        dst_rest = dst[FULL * GROUP:E].rearrange("(a e) -> a e", a=1)
        dst_tiles = dst[0:ET * SPAN].rearrange("(t e) -> t e", e=SPAN)

        def column(a):
            return a.rearrange("(p a) -> p a", a=1)

        def load_rest(eng, u0, loaded):
            for k in range(2):
                more = min(HALF, REST_E - k * HALF) * D
                eng.dma_start(edges[0:REST_P, u0 + k, :], edge_rest[:, k * HD:(k + 1) * HD]).then_inc(loaded, 16)
                eng.dma_start(edges[REST_P:REST_P + 1, u0 + k, 0:more],
                              edge_last[:, k * HD:k * HD + more]).then_inc(loaded, 16)

        block = ctx.enter_context(nc.Block())

        @block.sync
        def _(sp):
            sp.wait_ge(rows_padded, 2)
            sp.dma_start(rows_i[0:FULL, :], dst_full).then_inc(dst_loaded, 16)
            sp.dma_start(rows_i[FULL:GROUPS, 0:REST], dst_rest).then_inc(dst_loaded, 16)

            def load(g, k, u, free):
                sp.wait_ge(halves_free, free)
                sp.dma_start(edges[:, u, :], edge_full[g, :, k * HD:(k + 1) * HD]).then_inc(edge_loaded[u], 16)

            with sp.Fori(0, LEAD + CHUNKS) as r:
                for u in range(HPC):
                    load(r * GPC + u // 2, u % 2, u, r * HPC + (u + 1))
            for k in range(2):
                load(FULL - 1, k, k, 2 * (FULL - 1) + k + 1)
            sp.wait_ge(halves_free, 2 * FULL + 2)
            load_rest(sp, 2, tail_loaded)

            def general(n):
                sp.wait_ge(slots_clear, n + 1)
                sp.sem_inc(passes_begun, 1)

            def load_group(g, n):
                general(n)
                for k in range(2):
                    sp.dma_start(edges[:, k, :], edge_full[g, :, k * HD:(k + 1) * HD]).then_inc(group_loaded, 16)
                for to, a in ((edge_dst, dst), (edge_src, src)):
                    v = a[0:FULL * GROUP].rearrange("(g p j) -> g p j", p=P, j=TILES)
                    sp.dma_start(to[:, :], v[g, :, :]).then_inc(group_loaded, 16)
                for _ in range(4):
                    sp.sem_inc(group_loaded, 16)

            sp.wait_ge(mode_ready, 1)
            with sp.If(sp.value_load(flag_i[0:1, 0:1], min_val=0, max_val=1) > 0):
                with sp.Fori(0, PASSES) as w:
                    with sp.Fori(0, FULL) as g:
                        load_group(g, w * GROUPS + g)
                    general(w * GROUPS + FULL)
                    load_rest(sp, 0, group_loaded)
                    for to, a in ((edge_dst, dst), (edge_src, src)):
                        whole = a[rest0:rest0 + REST_P * TILES].rearrange("(p j) -> p j", j=TILES)
                        more = a[rest0 + REST_P * TILES:E].rearrange("(a j) -> a j", a=1)
                        sp.dma_start(to[0:REST_P, :], whole).then_inc(group_loaded, 16)
                        sp.dma_start(to[REST_P:REST_P + 1, 0:REST_E], more).then_inc(group_loaded, 16)

            sp.wait_ge(agg_ready, 1)
            sp.dma_start(xs[:, 0:NT - 1, :], x[0:(NT - 1) * P, :].rearrange("(t p) d -> p t d", p=P)
                         ).then_inc(xs_loaded, 16)
            sp.dma_start(xs[0:LAST, NT - 1, :], x[(NT - 1) * P:N, :]).then_inc(xs_loaded, 16)

            out_blocks = out[0:BLOCKS * BLOCK * P, :].rearrange("(k t p) d -> k p t d", p=P, t=2 * BLOCK)
            with sp.Fori(0, BLOCKS // 2) as k:
                sp.wait_ge(out_ready, 2 * (BLOCK - ACT_TILES) * (k + 1))
                sp.wait_ge(act_out_ready, 2 * ACT_TILES * (k + 1))
                sp.dma_start(out_blocks[k, :, :, :], xs[:, bass.ds(k * (2 * BLOCK), 2 * BLOCK), :]
                             ).then_inc(out_stored, 16)
            sp.wait_ge(out_ready, NT - ACT_TILES * BLOCKS)
            sp.dma_start(out[(NT - 1) * P:N, :], xs[0:LAST, NT - 1, :]).then_inc(out_stored, 16)
            sp.wait_ge(out_stored, 16 * (BLOCKS // 2 + 1))

        @block.gpsimd
        def _(pool):
            pool.iota(iota_i[:, :], [[1, P]], base=0, channel_multiplier=0)
            pool.iota(prow_i[:, :], [[0, 1]], base=0, channel_multiplier=1)
            pool.iota(pair_i[:, :], [[PAIR * PAIRS, CHUNKS + 1]], base=0, channel_multiplier=PAIR)
            pool.memset(ones_b[:, :], 1.0)
            pool.memset(ones[:, :], 1.0).then_inc(consts_ready, 1)
            half = SEARCH * PAIRS
            for at, to in ((0, half), (half, NPAIR + 7)):
                pool.iota(pair_row[:, at:to], [[1, to - at]], base=at, channel_multiplier=0,
                          allow_small_or_imprecise_dtypes=True).then_inc(pair_row_ready, 1)
            for s, places in ((halves_free, HALVES), (sums_copied, 3), (sums_turned, 3), (edges_added, 3),
                              (banks_done, CREDIT), (chunk_summed, 1), (chunk_added, 1)):
                pool.sem_inc(s, places)
            pool.wait_ge(setup, ROWS_READ)
            pool.wait_ge(turned, TILES // 4)
            pool.wait_ge(listed_stored, 48)
            pool.memset(agg[:, :], 0.0).then_inc(agg_zeroed, 1)
            pool.wait_ge(below_ready, 2 * SETS)
            pool.iota(values[:, :, :], [[1, P], [0, BP]], base=0, channel_multiplier=0,
                      allow_small_or_imprecise_dtypes=True).then_inc(pads_ready, 1)

            with pool.Fori(0, CHUNKS + 1) as c:
                pool.wait_ge(table_built, 16 * PARTS)
                pool.wait_ge(tile_staged, c + 1)
                pool.sem_inc(gathers_begun, 1)
                for k in range(2):
                    pool.indirect_dma_start(begins[0:PAIRS, k * P:(k + 1) * P], None, listed_rows,
                                            bass.IndirectOffsetOnAxis(tile_slot[0:PAIRS, k:k + 1], 0)
                                            ).then_inc(begins_loaded, 16)
                pool.wait_ge(row_staged, c + 1)
                pool.sem_inc(gathers_begun, 1)
                pool.indirect_dma_start(near[0:PAIRS, :], None, listed_rows,
                                        bass.IndirectOffsetOnAxis(row_slot[0:PAIRS, 0:1], 0)
                                        ).then_inc(near_loaded, 16)

            pool.wait_ge(mode_ready, 1)
            with pool.If(pool.value_load(flag_i[0:1, 0:1], min_val=0, max_val=1) > 0):
                with pool.Fori(0, PASSES * GROUPS) as n:
                    pool.wait_ge(group_loaded, (n + 1) * 128)
                    pool.sem_inc(gathers_begun, 1)
                    for j in range(TILES):
                        pool.indirect_dma_start(edges[:, 2 + j // HALF, (j % HALF) * D:(j % HALF + 1) * D], None, x,
                                                bass.IndirectOffsetOnAxis(edge_src[:, j:j + 1], 0)
                                                ).then_inc(group_gathered, 16)

        @block.scalar
        def _(act):
            act.wait_ge(rows_padded, 1)
            whole = (SETS - 1) * P
            with nc.allow_non_contiguous_dma("a word of each tile"):
                act.dma_start(tile_end_i[:, 0:SETS - 1],
                              dst_tiles[0:whole, SPAN - 1].rearrange("(s p) -> p s", p=P)).then_inc(ends_loaded, 16)
                act.dma_start(tile_end_i[0:ET - whole, SETS - 1:SETS],
                              dst_tiles[whole:ET, SPAN - 1:SPAN]).then_inc(ends_loaded, 16)
            act.wait_ge(rows_padded, 2)
            act.dma_start(src_rows[0:FULL, :], src[0:FULL * GROUP].rearrange("(g e) -> g e", e=GROUP)
                          ).then_inc(src_loaded, 16)
            act.dma_start(src_rows[FULL:GROUPS, 0:REST], src[FULL * GROUP:E].rearrange("(a e) -> a e", a=1)
                          ).then_inc(src_loaded, 16)
            act.wait_ge(rows_padded, 3)
            act.dma_start(x_raw[:, 0:(NT - 1) * D].rearrange("p (t d) -> p t d", d=D),
                          x[0:(NT - 1) * P, :].rearrange("(t p) d -> p t d", p=P)).then_inc(x_loaded, 16)
            act.dma_start(x_raw[0:LAST, (NT - 1) * D:NT * D], x[(NT - 1) * P:N, :]).then_inc(x_loaded, 16)
            act.dma_start(listed[E:LISTED].rearrange("(a e) -> a e", a=1), no_edges[:, 0:LISTED - E]
                          ).then_inc(listed_stored, 16)
            act.wait_ge(listed_ready, 1)
            act.dma_start(listed[0:FULL * GROUP].rearrange("(g e) -> g e", e=GROUP), src_rows[0:FULL, :]
                          ).then_inc(listed_stored, 16)
            act.dma_start(listed[FULL * GROUP:E].rearrange("(a e) -> a e", a=1), src_rows[FULL:GROUPS, 0:REST]
                          ).then_inc(listed_stored, 16)
            act.wait_ge(listed_stored, 48)

            def build_table(i):
                at, to = (ROWS * k // PARTS for k in (i, i + 1))
                act.dma_start(listed_rows[at:to, :], bass.AP(listed.tensor, at * STRIDE, [[STRIDE, to - at], [1, P]])
                              ).then_inc(table_built, 16)

            for i in range(AT_ONCE):
                build_table(i)
            for k, a in enumerate((b2, ln_w, ln_b, gn_w, gn_b, gn_ms)):
                act.dma_start(par[:, k:k + 1], column(a)).then_inc(params_loaded, 16)
            act.dma_start(w1[:, :], W1).then_inc(weights_loaded, 16)
            act.dma_start(w2[:, :, :], W2.rearrange("(c p) d -> p c d", p=P)).then_inc(weights_loaded, 16)
            for c in range(HC):
                act.dma_start(b1c[:, c:c + 1], column(b1[c * P:(c + 1) * P])).then_inc(weights_loaded, 16)
            act.wait_ge(x_loaded, 32)
            nc.scalar.copy(x_hi[:, :, :], x_raw.rearrange("p (t d) -> p t d", d=D)).then_inc(x_high, 1)

            def copy_sums(g, s):
                act.wait_ge(halves_free, g * 2 + (2 + HALVES))
                act.wait_ge(sums_turned, g + 3)
                nc.scalar.copy(sums[:, :], eps[s]).then_inc(sums_copied, 1)

            def three_copies(r):
                for j in range(GPC):
                    copy_sums(r * GPC + j, j)

            def copy_keys(c):
                act.wait_ge(marks_ready, c * BATCHES)
                act.wait_ge(keys_turned, c + 1)
                for at, to in ((LO0, turned_lo), (KEY0, turned_key)):
                    nc.scalar.copy(to[:, :, 0:BATCH], turn_ps[:, at:at + PAIRS].rearrange("p (b n) -> p b n", n=BATCH)
                                   ).then_inc(keys_ready, 1)

            for g in range(LEAD0 * GPC):
                copy_sums(g, g % GPC)
                build_table(g + AT_ONCE)
            with act.Fori(LEAD0, LEAD - 2) as r:
                three_copies(r)
            act.wait_ge(pads_ready, 2)
            act.wait_ge(keys_turned, 1)
            for at, to in ((LO0, turned_lo), (KEY0, turned_key)):
                nc.scalar.copy(to[:, :, 0:BATCH], turn_ps[:, at:at + PAIRS].rearrange("p (b n) -> p b n", n=BATCH)
                               ).then_inc(keys_ready, 1)
            for r in range(LEAD - 2, LEAD):
                three_copies(r)

            def copy_chunk(c):
                act.wait_ge(chunk_summed, c + 1)
                for k in range(BANKS):
                    act.wait_ge(banks_done, c * BANKS + (k + 1 + CREDIT))
                    nodes = BANK * PAIR
                    nc.scalar.copy(counts[:, :, k * nodes:(k + 1) * nodes].rearrange("p q n -> p n q"),
                                   cps[k % RING][:, 0:nodes * NT].rearrange("p (n q) -> p n q", q=NT)
                                   ).then_inc(banks_free, 1)
                    if k in (10, 18, 24):
                        j = (10, 18, 24).index(k)
                        copy_sums(c * GPC + (LEAD * GPC + j), j)
                    if k == KEYS_AT:
                        copy_keys(c + 1)

            with act.Fori(0, CHUNKS) as c:
                copy_chunk(c)
            copy_sums(FULL - 1, 0)
            copy_sums(FULL, 1)

            act.wait_ge(mode_ready, 1)
            with act.If(act.value_load(flag_i[0:1, 0:1], min_val=0, max_val=1) > 0):
                with act.Fori(0, PASSES * GROUPS) as n:
                    act.wait_ge(group_summed, n + 1)
                    nc.scalar.copy(sums[:, :], eps[0]).then_inc(group_copied, 1)

            act.wait_ge(weights_loaded, 16 * (2 + HC))

            def relu(u, count):
                act.wait_ge(z_ready, count)
                for c in range(HC):
                    nc.scalar.activation(hidden[:, u, c, :], zps[u][:, c, 0:CHUNK], ACT.Relu,
                                         bias=b1c[:, c:c + 1]).then_inc(hidden_ready, 1)

            with act.Fori(0, CHUNKS // 2) as it:
                for u in range(2):
                    relu(u, it * 2 + (u + 1))
            relu(0, CHUNKS)
            for k, (a, b) in enumerate(((st[:, 4:5], turn_ps[:, 1:2]), (st[:, 9:10], st[:, 9:10]))):
                act.wait_ge(root_in, k + 1)
                nc.scalar.activation(a, b, ACT.Sqrt, bias=st[:, 21:22]).then_inc(root_out, 1)

            act.wait_ge(affine_ready, 1)

            def activate(k, u, free, width):
                if free is not None:
                    act.wait_ge(out_turned, free)
                nc.scalar.activation(gelu[:, u, 0:width], h[:, bass.ds(k * (BLOCK * P), width)],
                                     ACT.Gelu_apprx_tanh, scale=st[:, 10:11], bias=st[:, 12:13]
                                     ).then_inc(act_ready, 1)

            activate(0, 0, None, BLOCK * P)
            activate(1, 1, None, BLOCK * P)
            with act.Fori(1, BLOCKS // 2) as it:
                for u in range(2):
                    activate(it * 2 + u, u, it * 2 + (u - 1), BLOCK * P)
            activate(BLOCKS, 0, BLOCKS - 1, LAST)
            act.wait_ge(root_in, 3)
            nc.scalar.activation(rstd[:, :], rstd[:, :], ACT.Sqrt).then_inc(root_out, 1)

            act.wait_ge(scales_ready, 1)
            with act.Fori(0, BLOCKS // OPS) as k:
                for u in range(OPS):
                    for t in range(ACT_TILES):
                        at = bass.ds(k * (OPS * BLOCK) + (u * BLOCK + t), 1)
                        yt = xs[:, at, :].rearrange("p a d -> p (a d)")
                        nc.scalar.activation(yt, yt, ACT.Identity, scale=rstd[:, at], bias=lnmean_act[:, at]
                                             ).then_inc(act_out_ready, 1)

        @block.tensor
        def _(pe):
            def search(steps):
                for i in steps:
                    pe.wait_ge(below_ready, i + 1)
                    for c in range(i % 2 * SEARCH, min(CHUNKS, (i % 2 + 1) * SEARCH)):
                        at = (c - i % 2 * SEARCH) * PAIRS
                        last = nc.tensor.matmul(turn_ps[0:PAIRS, c:c + 1], below[:, i % BELOW, at:at + PAIRS],
                                                ones_b[:, :], start=(c == 0 and i == 0), stop=(i // 2 == SETS - 1),
                                                skip_group_check=True)
                    last.then_inc(below_used, 1)

            search(range(0, DST_AT + 3))
            pe.wait_ge(consts_ready, 2)
            pe.wait_ge(diag_ready, 1)
            for k in range(2):
                last = nc.tensor.matmul(sps[:, k * P:(k + 1) * P], ones[:, :], diag[:, k, :],
                                        start=(k == 0), stop=(k == 1), skip_group_check=True)
            last.then_inc(base_summed, 1)
            pe.wait_ge(rows_ready, 1)
            rows = rows_f.rearrange("g (p j) -> g p j", j=TILES)
            for j in range(TILES):
                last = nc.tensor.transpose(banks[j // 4][:, (j % 4) * P:(j % 4) * P + GROUPS], rows[0:GROUPS, :, j],
                                           ident[0:GROUPS, 0:GROUPS])
                if j % 4 == 3:
                    last.then_inc(turned, 1)
            search(range(DST_AT + 3, 2 * SETS))

            def sum_tiles(u, s, k, tiles):
                oh = onehot[:, u % PLACES, :].rearrange("p (j w) -> p j w", w=WINDOW)
                for j in tiles:
                    last = nc.tensor.matmul(eps[s], oh[:, j, :], edges[:, u, j * D:(j + 1) * D],
                                            start=(k == 0 and j == 0), stop=(k == 1 and j == HALF - 1),
                                            skip_group_check=True)
                if tiles[-1] == HALF - 1:
                    last.then_inc(halves_free, 1)

            def begin_half(g, k, loaded, count):
                pe.wait_ge(onehot_ready, g * 2 + (k + 1))
                if k == 0:
                    pe.wait_ge(edges_added, g + 1)
                pe.wait_ge(loaded, count)

            def turn_sums(g, s):
                pe.wait_ge(sums_copied, g + 4)
                nc.tensor.transpose(turned_sum[s], sums[:, :], ident[0:WINDOW, 0:WINDOW]
                                    ).then_inc(sums_turned, 1)

            def three_groups(r, first=False):
                for j in range(GPC):
                    for k in range(2):
                        u = 2 * j + k
                        begin_half(r * GPC + j, k, edge_loaded[u], r * 16 + 16)
                        sum_tiles(u, j, k, range(HALF))
                    if not (first and j == 0):
                        turn_sums(r * GPC + (j - 1), (j - 1) % 3)

            for r in range(LEAD0):
                three_groups(r, r == 0)
            with pe.Fori(LEAD0, LEAD - 2) as r:
                three_groups(r)

            def turn_keys(c):
                pe.wait_ge(keys_made, c + 1)
                for at, rows in ((LO0, lo_f), (KEY0, node_f)):
                    last = nc.tensor.transpose(turn_ps[:, at:at + PAIRS], rows[0:PAIRS, :], ident[0:PAIRS, 0:PAIRS])
                last.then_inc(keys_turned, 1)

            turn_keys(0)
            for r in range(LEAD - 2, LEAD):
                three_groups(r)

            def count_chunk(c):
                tiles = HPC * HALF // (BANKS - 1)
                for k in range(BANKS):
                    b = k // BPB
                    if k % BPB == 0:
                        pe.wait_ge(marks_ready, c * BATCHES + (b + 1))
                    if k >= RING:
                        pe.wait_ge(banks_free, c * BANKS + (k + 1 - RING))
                    for i in range(BANK):
                        n = (k % BPB) * BANK + i
                        last = nc.tensor.matmul(cps[k % RING][:, i * KEYS:(i + 1) * KEYS], mark_lo[b % MARKED][:, :, n],
                                                mark_key[b % MARKED][:, :, n], start=(i == 0), stop=(i == BANK - 1),
                                                skip_group_check=True)
                    last.then_inc(banks_done, 1)
                    for t in range((k - 2) * tiles, (k - (k < BANKS - 1)) * tiles, tiles) if k >= 2 else ():
                        u = t // HALF
                        g = c * GPC + (LEAD * GPC + u // 2)
                        if t % HALF == 0:
                            begin_half(g, u % 2, edge_loaded[u], (c + LEAD) * 16 + 16)
                        sum_tiles(u, u // 2, u % 2, range(t % HALF, t % HALF + tiles))
                        if (t + tiles) % (2 * HALF) == 0:
                            turn_sums(g - 1, (u // 2 - 1) % 3)
                    if k == KEYS_AT:
                        pe.wait_ge(keys_ready, c * 2 + 2)
                        turn_keys(c + 1)
                pe.wait_ge(banks_free, (c + 1) * BANKS)
                pe.wait_ge(chunk_added, c + 1)
                for q in range(NT):
                    for part in (x_hi, x_lo):
                        last = nc.tensor.matmul(sps[:, 0:CHUNK], part[:, q, :], counts[:, q, :],
                                                start=(q == 0 and part is x_hi), stop=(q == NT - 1 and part is x_lo))
                last.then_inc(chunk_summed, 1)

            pe.wait_ge(x_split, NT // PIECE)
            with pe.Fori(0, CHUNKS) as c:
                count_chunk(c)
            pe.wait_ge(cover_in, 1)
            pe.wait_ge(keys_ready, 2 * (CHUNKS + 1))
            nc.tensor.matmul(turn_ps[:, 0:1], ones[:, :], st[:, 20:21], start=True, stop=True
                             ).then_inc(cover_summed, 1)
            for g, loaded, count in ((FULL - 1, edge_loaded, (LEAD + CHUNKS) * 16 + 16), (FULL, None, 64)):
                for k in range(2):
                    u = 2 * (g - FULL + 1) + k
                    begin_half(g, k, loaded[u] if loaded else tail_loaded, count)
                    sum_tiles(u, g - FULL + 1, k, range(HALF))
                turn_sums(g - 1, (g - 1) % 3)
            turn_sums(FULL, 1)

            pe.wait_ge(mode_ready, 1)
            with pe.If(pe.value_load(flag_i[0:1, 0:1], min_val=0, max_val=1) > 0):
                with pe.Fori(0, PASSES * GROUPS) as n:
                    pe.wait_ge(group_marked, n + 1)
                    pe.wait_ge(group_gathered, (n + 1) * (16 * TILES))
                    for i in range(4):
                        oh = onehot[:, i % 2, :].rearrange("p (j w) -> p j w", w=WINDOW)
                        for j in range(HALF):
                            last = nc.tensor.matmul(eps[0], oh[:, j, :], edges[:, i, j * D:(j + 1) * D],
                                                    start=(i == 0 and j == 0), stop=(i == 3 and j == HALF - 1))
                    last.then_inc(group_summed, 1)
                    pe.wait_ge(group_copied, n + 1)
                    nc.tensor.transpose(turned_sum[0], sums[:, :], ident[0:WINDOW, 0:WINDOW]
                                        ).then_inc(group_turned, 1)
            pe.wait_ge(agg_ready, 1)
            pe.wait_ge(weights_loaded, 16 * (2 + HC))

            def up(c, u, free):
                if free is not None:
                    pe.wait_ge(hidden_ready, free)
                for k in range(HC):
                    last = nc.tensor.matmul(zps[u][:, k, 0:CHUNK], w1[:, k * P:(k + 1) * P],
                                            agg[:, bass.ds(c * CHUNK, CHUNK)], start=True, stop=True,
                                            skip_group_check=True)
                last.then_inc(z_ready, 1)

            def down(u, count, free):
                pe.wait_ge(hidden_ready, count)
                if free is not None:
                    pe.wait_ge(h_ready, free)
                for k in range(HC):
                    last = nc.tensor.matmul(hps[u][:, 0:CHUNK], w2[:, k, :], hidden[:, u, k, :],
                                            start=(k == 0), stop=(k == HC - 1))
                last.then_inc(h_summed, 1)

            up(0, 0, None)
            up(1, 1, None)
            down(0, HC, None)
            up(2, 0, HC)
            down(1, 2 * HC, None)
            with pe.Fori(0, (CHUNKS - 3) // 2) as it:
                for u in range(2):
                    up(it * 2 + (u + 3), 1 - u, it * (2 * HC) + (u + 2) * HC)
                    down(u, it * (2 * HC) + (u + 3) * HC, it * 2 + (u + 1))
            down(0, CHUNKS * HC, CHUNKS - 2)

            for k in range(2):
                pe.wait_ge(mean_in, k + 1)
                nc.tensor.matmul(turn_ps[:, k:k + 1], ones[:, :], st[:, k:k + 1],
                                 start=True, stop=True, skip_group_check=True).then_inc((mean_summed, root_in)[k], 1)

            def turn(u, count, free):
                pe.wait_ge(act_ready, count)
                if free is not None:
                    pe.wait_ge(y_ready, free)
                for t in range(BLOCK):
                    last = nc.tensor.transpose(ops[u][:, t * P:(t + 1) * P], gelu[:, u % 2, t * P:(t + 1) * P],
                                               ident[:, :])
                last.then_inc(out_turned, 1)

            for u in range(OPS):
                turn(u, u + 1, None)
            with pe.Fori(1, BLOCKS // OPS) as it:
                for u in range(OPS):
                    turn(u, it * OPS + (u + 1), it * OPS + (u + 1 - OPS))
            pe.wait_ge(act_ready, BLOCKS + 1)
            pe.wait_ge(y_ready, BLOCKS + 1 - OPS)
            nc.tensor.transpose(ops[0][0:LAST, 0:P], gelu[:, 0, 0:LAST], ident[:, :]).then_inc(out_turned, 1)

        @block.vector
        def _(dve):
            steps = [0]

            def link(ins, chain, count):
                count[0] += 1
                ins.then_inc(chain, 1)
                dve.wait_ge(chain, count[0])

            link(dve.memset(tile_end_i[:, :], 2 * N), setup, steps)
            dve.engine_nop().then_inc(rows_padded, 1)
            dve.memset(src_rows[96:P, REST:GROUP], 0)
            link(dve.memset(rows_i[96:P, REST:GROUP], -1), setup, steps)
            dve.engine_nop().then_inc(rows_padded, 1)
            dve.memset(no_edges[:, :], NO_EDGE)
            link(dve.memset(x_raw[96:P, (NT - 1) * D:NT * D], 0.0), setup, steps)
            dve.engine_nop().then_inc(rows_padded, 1)
            dve.memset(lo[:, :], 0.0)
            link(dve.memset(hi[:, :], 0.0), setup, steps)
            dve.wait_ge(consts_ready, 1)
            dve.tensor_copy(iota_f[:, :], iota_i[:, :])
            dve.tensor_copy(pair_f[:, :], pair_i[:, :])
            link(dve.tensor_copy(prow_f[:, :], prow_i[:, :]), setup, steps)
            dve.tensor_scalar(pair_w[:, :], pair_f[:, :], float(1 << DST_SHIFT), None, ALU.mult)
            dve.tensor_scalar(ident[:, :], iota_f[:, :], prow_f[:, 0:1], None, ALU.is_equal
                              ).then_inc(consts_ready, 1)
            dve.wait_ge(ends_loaded, 32)
            link(dve.tensor_scalar(tile_end[:, :], tile_end_i[:, :], 1.0 / PAIR, None, ALU.mult), setup, steps)

            def search(i):
                if i < 2:
                    dve.wait_ge(pair_row_ready, i + 1)
                if i >= BELOW:
                    dve.wait_ge(below_used, i + 1 - BELOW)
                v = range(i % 2 * SEARCH * PAIRS, min(NPAIR, (i % 2 + 1) * SEARCH * PAIRS))
                dve.tensor_scalar(below[:, i % BELOW, 0:len(v)], pair_row[:, v[0]:v[-1] + 1],
                                  tile_end[:, i // 2:i // 2 + 1], None, ALU.is_gt).then_inc(below_ready, 1)

            for i in range(0, DST_AT):
                search(i)

            dve.wait_ge(dst_loaded, 32)
            link(dve.tensor_copy(rows_f[0:GROUPS, :], rows_i[0:GROUPS, :]), setup, steps)
            search(DST_AT)
            dve.tensor_reduce(hi[0:GROUPS, :], rows_f[0:GROUPS, :], AX_X, ALU.max)
            link(dve.tensor_scalar(pad_f[0:GROUPS, :], rows_f[0:GROUPS, REST:GROUP], 0.0, PAD,
                                   ALU.is_lt, ALU.mult), setup, steps)
            link(dve.tensor_tensor(rows_f[0:GROUPS, REST:GROUP], rows_f[0:GROUPS, REST:GROUP],
                                   pad_f[0:GROUPS, :], ALU.add), setup, steps)
            dve.engine_nop().then_inc(rows_ready, 1)
            search(DST_AT + 1)
            link(dve.tensor_reduce(lo[0:GROUPS, :], rows_f[0:GROUPS, :], AX_X, ALU.min), setup, steps)
            assert steps[0] == ROWS_READ
            search(DST_AT + 2)
            link(dve.tensor_tensor(hi[:, :], hi[:, :], lo[:, :], ALU.subtract), setup, steps)
            dve.tensor_scalar(diag[:, 0, :], ident[:, :], lo[:, 0:1], None, ALU.mult)
            dve.tensor_scalar(diag[:, 1, :], ident[:, :], hi[:, 0:1], None, ALU.mult).then_inc(diag_ready, 1)
            search(DST_AT + 3)
            dve.wait_ge(src_loaded, 32)
            dve.scalar_tensor_tensor(src_rows[0:GROUPS, :], rows_i[0:GROUPS, :], DST_SHIFT, src_rows[0:GROUPS, :],
                                     ALU.logical_shift_left, ALU.bitwise_or).then_inc(listed_ready, 1)
            search(DST_AT + 4)

            dve.wait_ge(base_summed, 1)
            dve.tensor_copy(base_i[:, :], sps[0:1, 0:P])
            dve.tensor_copy(base_f[:, :], sps[:, 0:P])
            link(dve.tensor_reduce(wide[:, 0:1], sps[:, P:2 * P], AX_X, ALU.max), setup, steps)

            for q in range(TILES // 4):
                dve.wait_ge(turned, q + 1)
                dve.tensor_tensor(dst_cols[:, q * 4:q * 4 + 4, :],
                                  banks[q][:, :].rearrange("p (j g) -> p j g", g=P)[:, :, 0:GROUPS],
                                  base_f[:, 0:GROUPS].rearrange("p (a g) -> p a g", a=1).to_broadcast([P, 4, GROUPS]),
                                  ALU.subtract).then_inc(setup, 1)
            steps[0] += TILES // 4
            dve.wait_ge(setup, steps[0])

            window = iota_f[:, 0:WINDOW].rearrange("p (a w) -> p a w", a=1).to_broadcast([P, HALF, WINDOW])

            def mark(g, k, j):
                dve.wait_ge(halves_free, g * 2 + (k + HALVES + 1 - PLACES))
                oh = onehot[:, (2 * j + k) % PLACES, :].rearrange("p (j w) -> p j w", w=WINDOW)
                dve.tensor_tensor(oh, window, dst_cols[:, k * HALF:(k + 1) * HALF, bass.ds(g, 1)
                                                       ].to_broadcast([P, HALF, WINDOW]),
                                  ALU.is_equal).then_inc(onehot_ready, 1)

            def base_of(g):
                return dve.value_load(base_i[0:1, bass.ds(g, 1)], min_val=0, max_val=N - 1)

            def add(g, s, base, chunks=None):
                dve.wait_ge(sums_turned, g + 4)
                dve.wait_ge(edges_added, g + 3)
                if chunks is not None:
                    dve.wait_ge(chunk_added, chunks)
                at = agg[:, bass.ds(base, WINDOW)]
                dve.tensor_tensor(at, at, turned_sum[s], ALU.add).then_inc(edges_added, 1)

            def three_groups(r, first=False, batches=0):
                for j in range(GPC):
                    mark(r * GPC + j, 0, j)
                    if not first:
                        add(r * GPC + (j - GPC), j, base_of(r * GPC + (j - GPC)))
                    mark(r * GPC + j, 1, j)
                    if GPC - 1 - batches <= j < GPC - 1:
                        mark_batch(0, j - (GPC - 1 - batches))

            def split_x(i):
                at = bass.ds(i * PIECE, PIECE)
                dve.tensor_tensor(x_lo[:, at, :], xs[:, at, :], x_hi[:, at, :].bitcast(F32), ALU.subtract
                                  ).then_inc(x_split, 1)

            for i in range(DST_AT + 5, 2 * SETS):
                search(i)
                if i == DST_AT + 6:
                    dve.memset(tile_f[:, :], 0.0)
                    dve.memset(turned_lo[:, :, :], -1.0)
                    link(dve.memset(turned_key[:, :, :], -1.0), setup, steps)
                    dve.engine_nop().then_inc(pads_ready, 1)
            three_groups(0, True)
            dve.wait_ge(below_used, 2 * SETS)
            link(dve.tensor_copy(tile_f[0:PAIRS, 0:CHUNKS], turn_ps[0:PAIRS, 0:CHUNKS]), setup, steps)
            for k in range(2):
                link(dve.tensor_scalar(tile_rows[:, :, k], tile_f[:, :], float(SPAN // STRIDE),
                                       float(k * P // STRIDE), ALU.mult, ALU.add), setup, steps)
            dve.wait_ge(agg_zeroed, 1)
            three_groups(1)
            dve.wait_ge(x_high, 1)
            split_x(0)

            def prep_chain(ins, count):
                ins.then_inc(prep, 1)
                dve.wait_ge(prep, count)

            STEPS = 9

            def stage_tile(c):
                dve.tensor_copy(tile_slot[0:PAIRS, :], tile_rows[0:PAIRS, bass.ds(c, 1), :].rearrange(
                    "p a k -> p (a k)")).then_inc(tile_staged, 1)

            def stage_row(c):
                dve.wait_ge(begins_loaded, c * 32 + 32)
                n = c * STEPS
                prep_chain(dve.tensor_scalar(junk[0:PAIRS, :], begins[0:PAIRS, :], pair_w[0:PAIRS, bass.ds(c, 1)], 0.0,
                                             ALU.is_lt, ALU.add, accum_out=first_f[0:PAIRS, :]), n + 1)
                prep_chain(dve.scalar_tensor_tensor(first_i[0:PAIRS, :], tile_f[0:PAIRS, bass.ds(c, 1)], float(SPAN),
                                                    first_f[0:PAIRS, :], ALU.mult, ALU.add), n + 2)
                dve.tensor_scalar(row_slot[0:PAIRS, :], first_i[0:PAIRS, :], 4, None, ALU.arith_shift_right
                                  ).then_inc(row_staged, 1)

            def make_keys(c):
                dve.wait_ge(near_loaded, c * 16 + 16)
                n = c * STEPS + 2
                w = near[0:PAIRS, :]
                dve.tensor_scalar(lo_i[0:PAIRS, :], w, P - 1, None, ALU.bitwise_and).then_inc(prep, 1)
                dve.tensor_scalar(hi_i[0:PAIRS, :], w, SHIFT, (1 << DST_SHIFT - SHIFT) - 1, ALU.arith_shift_right,
                                  ALU.bitwise_and).then_inc(prep, 1)
                prep_chain(dve.tensor_scalar(node_i[0:PAIRS, :], w, DST_SHIFT, None, ALU.arith_shift_right), n + 3)
                prep_chain(dve.tensor_scalar(node_f[0:PAIRS, :], node_i[0:PAIRS, :], pair_f[0:PAIRS, bass.ds(c, 1)], None,
                                             ALU.subtract), n + 4)
                dve.scalar_tensor_tensor(junk[0:PAIRS, 0:P], node_f[0:PAIRS, :], -1.0, node_f[0:PAIRS, :],
                                         ALU.add, ALU.mult).then_inc(prep, 1)
                dve.tensor_copy(lo_f[0:PAIRS, :], lo_i[0:PAIRS, :]).then_inc(prep, 1)
                prep_chain(dve.scalar_tensor_tensor(node_f[0:PAIRS, :], node_f[0:PAIRS, :], float(NT), hi_i[0:PAIRS, :],
                                                    ALU.mult, ALU.add), n + 7)
                dve.tensor_scalar(junk[0:PAIRS, 0:P], junk[0:PAIRS, 0:P], 0.0, 0.0, ALU.is_equal, ALU.add,
                                  accum_out=covered[0:PAIRS, bass.ds(c, 1)]).then_inc(keys_made, 1)
                dve.wait_ge(keys_made, c + 1)

            def mark_batch(c, b):
                if b == 0:
                    dve.wait_ge(keys_ready, c * 2 + 2)
                if b < BATCHES - MARKED:
                    dve.wait_ge(banks_done, c * BANKS + ((b + MARKED + 1) * BPB - BANKS + CREDIT))
                elif b >= MARKED:
                    dve.wait_ge(banks_done, c * BANKS + ((b - MARKED + 1) * BPB + CREDIT))
                for rows, to, n in ((turned_lo, mark_lo, P), (turned_key, mark_key, KEYS)):
                    last = dve.tensor_tensor(to[b % MARKED], values[:, 0:n, :],
                                             rows[:, b:b + 1, :].to_broadcast([P, n, BP]), ALU.is_equal)
                last.then_inc(marks_ready, 1)

            stage_tile(0)
            with dve.Fori(2, LEAD - 3) as r:
                three_groups(r)
                split_x(r - 1)
            stage_row(0)
            three_groups(LEAD - 3)
            split_x(LEAD - 4)
            split_x(LEAD - 3)
            make_keys(0)
            three_groups(LEAD - 2)
            split_x(LEAD - 2)
            dve.wait_ge(x_split, NT // PIECE)
            dve.wait_ge(pads_ready, 2)
            three_groups(LEAD - 1, batches=2)

            def head(c, chunks):
                g = c * GPC + LEAD * GPC
                stage_tile(c + 1)
                if chunks is not None:
                    mark_batch(c, 0)
                mark(g, 0, 0)
                base = base_of(g - GPC)
                if chunks is not None:
                    mark_batch(c, 1)
                add(g - GPC, 0, base, chunks)
                mark(g, 1, 0)
                mark_batch(c, 2)
                mark(g + 1, 0, 1)

            def rest(c, before, groups):
                g = c * GPC + LEAD * GPC
                base = base_of(g + (1 - GPC))
                if before is not None:
                    add_chunk(before, groups)
                stage_row(c + 1)
                add(g + (1 - GPC), 1, base, c + 1)
                mark_batch(c, 3)
                mark(g + 1, 1, 1)
                base = base_of(g + (2 - GPC))
                mark_batch(c, 4)
                add(g + (2 - GPC), 2, base)
                mark(g + 2, 0, 2)
                make_keys(c + 1)
                mark(g + 2, 1, 2)

            def add_chunk(c, groups):
                dve.wait_ge(chunk_summed, c + 2)
                dve.wait_ge(edges_added, groups + 3)
                at = agg[:, bass.ds(c * CHUNK, CHUNK)]
                dve.tensor_tensor(at, at, sps[:, 0:CHUNK], ALU.add).then_inc(chunk_added, 1)

            head(0, None)
            rest(0, None, None)
            with dve.Fori(1, CHUNKS) as c:
                head(c, c)
                rest(c, c - 1, c * GPC + (LEAD * GPC - 2))

            steps = [0]

            def step(ins):
                link(ins, norm, steps)

            dve.memset(st[:, 21:22], EPS)
            step(dve.memset(st[:, 20:21], 0.0))
            step(dve.tensor_reduce(st[0:PAIRS, 20:21], covered[0:PAIRS, :], AX_X, ALU.add))
            dve.engine_nop().then_inc(cover_in, 1)
            for g in (FULL - 1, FULL):
                mark(g, 0, g % GPC)
                add(g - 3, (g - 3) % 3, base_of(g - 3), CHUNKS)
                mark(g, 1, g % GPC)
            dve.wait_ge(cover_summed, 1)
            step(dve.tensor_scalar(wide[:, 1:2], turn_ps[:, 0:1], float(E), None, ALU.not_equal))
            step(dve.tensor_scalar(wide[:, 0:1], wide[:, 0:1], float(WINDOW), None, ALU.is_ge))
            step(dve.tensor_tensor(wide[:, 0:1], wide[:, 0:1], wide[:, 1:2], ALU.max))
            step(dve.tensor_copy(flag_i[:, :], wide[0:1, 0:1]))
            dve.engine_nop().then_inc(mode_ready, 1)
            flag = dve.value_load(flag_i[0:1, 0:1], min_val=0, max_val=1)
            add_chunk(CHUNKS - 1, FULL - 2)
            dve.wait_ge(chunk_added, CHUNKS + 1)
            for g in range(FULL - 2, GROUPS):
                add(g, g % 3, base_of(g))
            dve.wait_ge(edges_added, GROUPS + 3)

            with dve.If(flag > 0):
                dve.memset(agg[:, :], 0.0).then_inc(agg_clear, 1)
                dve.memset(pass_base[:, :], -float(WINDOW)).then_inc(agg_clear, 1)
                dve.wait_ge(agg_clear, 2)
                with dve.Fori(0, PASSES) as w:
                    dve.tensor_scalar(pass_base[:, :], pass_base[:, :], float(WINDOW), None, ALU.add
                                      ).then_inc(agg_clear, 1)
                    dve.wait_ge(agg_clear, w + 3)
                    dve.sem_inc(passes_begun, 1)
                    with dve.Fori(0, GROUPS) as g:
                        n = w * GROUPS + g
                        dve.memset(edge_dst[:, :], -1)
                        dve.memset(edge_src[:, :], 0).then_inc(slots_clear, 1)
                        dve.wait_ge(group_loaded, (n + 1) * 128)
                        dve.tensor_scalar(edge_dst_f[:, :], edge_dst[:, :], pass_base[:, 0:1], None, ALU.subtract
                                          ).then_inc(gchain, 1)
                        dve.wait_ge(gchain, n + 1)
                        for k in range(2):
                            oh = onehot[:, k, :].rearrange("p (j w) -> p j w", w=WINDOW)
                            near_k = edge_dst_f[:, k * HALF:(k + 1) * HALF].rearrange("p (j a) -> p j a", a=1)
                            last = dve.tensor_tensor(oh, window, near_k.to_broadcast([P, HALF, WINDOW]), ALU.is_equal)
                        last.then_inc(group_marked, 1)
                        dve.wait_ge(group_turned, n + 1)
                        at = agg[:, bass.ds(w * WINDOW, WINDOW)]
                        dve.tensor_tensor(at, at, turned_sum[0], ALU.add).then_inc(group_added, 1)
                        dve.wait_ge(group_added, n + 1)
            dve.engine_nop().then_inc(agg_ready, 1)

            dve.wait_ge(params_loaded, 16 * 6)
            def keep(c, u, count):
                hc = h[:, bass.ds(c * CHUNK, CHUNK)]
                dve.wait_ge(h_summed, count)
                dve.tensor_scalar(hc, hps[u][:, 0:CHUNK], par[:, B2:B2 + 1], None, ALU.add).then_inc(h_ready, 1)
                dve.wait_ge(h_ready, count)
                dve.bn_stats(stats[:, bass.ds(c, 1), :].rearrange("p a s -> p (a s)"), hc).then_inc(h_stats, 1)

            with dve.Fori(0, CHUNKS // 2) as it:
                for u in range(2):
                    keep(it * 2 + u, u, it * 2 + (u + 1))
            keep(CHUNKS - 1, 0, CHUNKS)
            dve.wait_ge(h_stats, CHUNKS)

            def c(k):
                return st[:, k:k + 1]

            m, v = mv[:, 0:1], mv[:, 1:2]
            step(dve.bn_aggr(mv[:, :], stats[:, :, :].rearrange("p c s -> p (c s)")))
            dve.tensor_scalar(c(0), m, 1.0 / D, None, ALU.mult).then_inc(mean_in, 1)
            dve.wait_ge(mean_summed, 1)
            step(dve.tensor_tensor(c(2), m, turn_ps[:, 0:1], ALU.subtract))
            step(dve.tensor_tensor(c(3), c(2), c(2), ALU.mult))
            step(dve.tensor_tensor(c(3), c(3), v, ALU.add))
            dve.tensor_scalar(c(1), c(3), 1.0 / D, None, ALU.mult).then_inc(mean_in, 1)
            dve.wait_ge(root_out, 1)
            step(dve.reciprocal(c(4), c(4)))
            step(dve.tensor_tensor(c(5), c(4), par[:, LNW:LNW + 1], ALU.mult))
            step(dve.tensor_scalar(c(6), c(2), c(5), par[:, LNB:LNB + 1], ALU.mult, ALU.add))
            step(dve.tensor_tensor(c(7), c(6), par[:, GNM:GNM + 1], ALU.mult))
            step(dve.tensor_tensor(c(7), c(6), c(7), ALU.subtract))
            step(dve.tensor_tensor(c(8), c(7), c(7), ALU.mult))
            step(dve.tensor_tensor(c(9), c(5), c(5), ALU.mult))
            dve.scalar_tensor_tensor(c(9), v, c(9), c(8), ALU.mult, ALU.add).then_inc(root_in, 1)
            step(dve.tensor_tensor(c(10), c(5), m, ALU.mult))
            step(dve.tensor_tensor(c(10), c(7), c(10), ALU.subtract))
            step(dve.tensor_tensor(c(11), c(10), par[:, GNW:GNW + 1], ALU.mult))
            step(dve.tensor_tensor(c(13), c(5), par[:, GNW:GNW + 1], ALU.mult))
            dve.wait_ge(root_out, 2)
            step(dve.reciprocal(c(9), c(9)))
            step(dve.tensor_tensor(c(10), c(13), c(9), ALU.mult))
            step(dve.tensor_scalar(c(12), c(11), c(9), par[:, GNB:GNB + 1], ALU.mult, ALU.add))
            dve.engine_nop().then_inc(affine_ready, 1)

            dve.wait_ge(xs_loaded, 32)

            def finish(t0, u, count, tiles, rows):
                y = xs[0:rows, bass.ds(t0, tiles), :]
                dve.wait_ge(out_turned, count)
                got = ops[u][0:rows, 0:tiles * P].rearrange("p (t d) -> p t d", d=P)
                dve.scalar_tensor_tensor(y, y, 2.0, got, ALU.mult, ALU.add).then_inc(y_ready, 1)

            def measure(t0, count, tiles, rows):
                dve.wait_ge(y_ready, count)
                for t in range(tiles):
                    dve.bn_stats(lnstats[0:rows, bass.ds(t0 + t, 1), :].rearrange("p a s -> p (a s)"),
                                 xs[0:rows, bass.ds(t0 + t, 1), :].rearrange("p a d -> p (a d)")
                                 ).then_inc(ln_stats, 1)

            dve.memset(lnstats[:, NT - 1, :], 1.0).then_inc(ln, 1)
            dve.wait_ge(ln, 1)
            with dve.Fori(0, BLOCKS // OPS) as it:
                for u in range(OPS + 1):
                    if u < OPS:
                        finish(it * (OPS * BLOCK) + u * BLOCK, u, it * OPS + (u + 1), BLOCK, P)
                    if u:
                        measure(it * (OPS * BLOCK) + (u - 1) * BLOCK, it * OPS + u, BLOCK, P)
            finish(NT - 1, 0, BLOCKS + 1, 1, LAST)
            measure(NT - 1, BLOCKS + 1, 1, LAST)
            dve.wait_ge(ln_stats, NT)

            steps = [1]

            def lnstep(ins):
                link(ins, ln, steps)

            even, odd = lnstats[:, :, 1], lnstats[:, :, 4]
            dve.tensor_tensor(lngap[:, :], even, odd, ALU.subtract)
            lnstep(dve.tensor_tensor(lnmean[:, :], even, odd, ALU.add))
            dve.tensor_scalar(lnmean[:, :], lnmean[:, :], 0.5, None, ALU.mult)
            dve.tensor_tensor(rstd[:, :], lnstats[:, :, 2], lnstats[:, :, 5], ALU.add)
            lnstep(dve.tensor_tensor(lngap[:, :], lngap[:, :], lngap[:, :], ALU.mult))
            dve.tensor_scalar(lngap[:, :], lngap[:, :], 0.25, EPS, ALU.mult, ALU.add)
            lnstep(dve.tensor_scalar(rstd[:, :], rstd[:, :], 1.0 / D, None, ALU.mult))
            dve.tensor_tensor(rstd[:, :], rstd[:, :], lngap[:, :], ALU.add).then_inc(root_in, 1)
            dve.wait_ge(root_out, 3)
            lnstep(dve.reciprocal(rstd[:, :], rstd[:, :]))

            def normalise(t, rows):
                yt = xs[0:rows, bass.ds(t, 1), :].rearrange("p a d -> p (a d)")
                dve.tensor_scalar(yt, yt, lnmean[0:rows, bass.ds(t, 1)], rstd[0:rows, bass.ds(t, 1)],
                                  ALU.subtract, ALU.mult).then_inc(out_ready, 1)

            lnstep(dve.scalar_tensor_tensor(lnmean_act[:, :], lnmean[:, :], -1.0, rstd[:, :], ALU.mult, ALU.mult))
            dve.engine_nop().then_inc(scales_ready, 1)
            with dve.Fori(0, BLOCKS // OPS) as k:
                for u in range(OPS):
                    for t in range(ACT_TILES, BLOCK):
                        normalise(k * (OPS * BLOCK) + (u * BLOCK + t), P)
            normalise(NT - 1, LAST)


_INS = ['x', 'src', 'dst', 'edge_attr_128', 'L0_gnn_W1', 'L0_gnn_b1', 'L0_gnn_W2', 'L0_gnn_b2', 'L0_gnn_ln_w',
        'L0_gnn_ln_b', 'L0_gnn_gn_w', 'L0_gnn_gn_b', 'L0_gnn_gn_ms']
_OUTS = [((6250, 128), 'float32')]


def kernel(**inputs):
    import numpy as _np
    import concourse.bacc as _bacc
    from concourse import mybir as _mybir
    from concourse.bass_utils import run_bass_kernel_spmd as _run

    nc = _bacc.Bacc("TRN2", target_bir_lowering=False, num_devices=1)
    arrays, args = {}, []
    for name in _INS:
        a = _np.ascontiguousarray(inputs[name])
        arrays[f"in_{name}_dram"] = a
        args.append(nc.dram_tensor(f"in_{name}_dram", a.shape, _mybir.dt.from_np(a.dtype), kind="ExternalInput").ap())
    for i, (shape, dtype) in enumerate(_OUTS):
        dt = _mybir.dt.from_np(_np.dtype(dtype))
        args.append(nc.dram_tensor(f"out_{i}_dram", shape, dt, kind="ExternalOutput").ap())
    gnn_kernel(nc, *args)
    r = _run(nc, [arrays], core_ids=[0])
    got = tuple(r.results[0][f"out_{i}_dram"] for i in range(len(_OUTS)))
    return got[0]
```
